# Optimizing a Trainium2 kernel written in Bass

```python
import numpy as np
import jax
import jax.numpy as jnp

def _softmax(x, axis=-1):
    return jax.nn.softmax(x, axis=axis)

def _gelu(x):
    return jax.nn.gelu(x, approximate=True)

def _silu(x):
    return jax.nn.silu(x)

def _sigmoid(x):
    return jax.nn.sigmoid(x)

def _layernorm(x, axis=-1, eps=1e-05):
    m = jnp.mean(x, axis=axis, keepdims=True)
    v = jnp.var(x, axis=axis, keepdims=True)
    return (x - m) / jnp.sqrt(v + eps)

def _scatter_add(tgt, idx, src, axis=0):
    return tgt.at[idx].add(src)

def _segment_sum(src, seg, n):
    return jax.ops.segment_sum(src, seg, n)
kernel_name = 'mk_adaln_ffn_d2_seqx_r8_81d26d'

def setup_inputs(seed: int=0):
    np.random.seed(seed)
    _w = jnp.asarray

    def _rec_inputs():
        import jax
        import jax.numpy as jnp
        _rk = jax.random.key(seed)
        x = -0.000125 + 0.9999 * jax.random.normal(jax.random.fold_in(_rk, 1), (8, 128, 512), jnp.float32)
        _lenS = 128 - jax.random.randint(jax.random.fold_in(_rk, 7), (8,), 0, max(1, 128 // 4) + 1, jnp.int32)
        _lenS2 = 128 - jax.random.randint(jax.random.fold_in(_rk, 8), (8,), 0, max(1, 128 // 4) + 1, jnp.int32)
        itok_B_0_23 = jax.random.randint(jax.random.fold_in(_rk, 11), (8,), 0, 24, jnp.int32)
        itok_B_0_15 = jax.random.randint(jax.random.fold_in(_rk, 12), (8,), 0, 16, jnp.int32)
        return (x, itok_B_0_23, itok_B_0_15)
    x, itok_B_0_23, itok_B_0_15 = _rec_inputs()

    def _L0_cond_setup():
        import jax, jax.numpy as jnp
        import numpy as np
        R = 16
        ALPHA = 32
        SCALING = ALPHA / R
        SLOTS = 32
        IN_F = 512
        OUT_F = 512
        B, T = (8, 128)
        key = jax.random.key(seed)
        k1, k2, k3, k4, k5, k6 = jax.random.split(key, 6)
        x = jax.random.normal(k1, (B, T, IN_F), dtype=jnp.float32)
        adapter_mapping = jax.random.randint(k2, (B,), 0, SLOTS, dtype=jnp.int32)
        W = jax.random.normal(k3, (OUT_F, IN_F), dtype=jnp.float32) * 0.02
        b = jax.random.normal(k4, (OUT_F,), dtype=jnp.float32) * 0.02
        lora_As = jax.random.normal(k5, (SLOTS, IN_F, R), dtype=jnp.float32) * 0.02
        lora_Bs = jax.random.normal(k6, (SLOTS, R, OUT_F), dtype=jnp.float32) * 0.02
        return {'x': x, 'adapter_mapping': adapter_mapping, 'W': W, 'b': b, 'lora_As': lora_As, 'lora_Bs': lora_Bs}
    _L0_cond_all = _L0_cond_setup()
    _L0_cond_in = {k: v for k, v in _L0_cond_all.items() if k in ('W', 'b', 'lora_As', 'lora_Bs')}
    del _L0_cond_all

    def _L0_ffn_setup():
        import jax, jax.numpy as jnp
        import numpy as np
        LORA_R = 16
        SCALE = 16.0 / np.sqrt(16.0)
        NUM_EXPERTS = 4
        TOP_K = 2
        IN_F = 512
        OUT_F = 512
        key = jax.random.key(seed)
        k_x, k_a, k_b, k_r = jax.random.split(key, 4)
        x = jax.random.normal(k_x, (2, 256, IN_F), dtype=jnp.float32)
        A = jax.random.normal(k_a, (NUM_EXPERTS, LORA_R, IN_F), dtype=jnp.float32) * (1.0 / np.sqrt(IN_F))
        B = jax.random.normal(k_b, (NUM_EXPERTS, OUT_F, LORA_R), dtype=jnp.float32) * 0.02
        Wr = jax.random.normal(k_r, (NUM_EXPERTS, IN_F), dtype=jnp.float32) * 0.02
        return {'x': x, 'A': A, 'B': B, 'Wr': Wr}
    _L0_ffn_all = _L0_ffn_setup()
    _L0_ffn_in = {k: v for k, v in _L0_ffn_all.items() if k in ('A', 'B', 'Wr')}
    del _L0_ffn_all

    def _L1_cond_setup():
        import jax, jax.numpy as jnp
        import numpy as np
        MAX_LORAS = 16
        IN, OUT = (512, 512)
        B, S = (8, 256)
        key = jax.random.key(seed)
        k1, k2, k3 = jax.random.split(key, 3)
        x = jax.random.normal(k1, (B, S, IN), dtype=jnp.float32)
        adapter_ids = jax.random.randint(k2, (B,), 0, MAX_LORAS)
        weight = jax.random.normal(k3, (MAX_LORAS, OUT, IN), dtype=jnp.float32) * 0.02
        return {'x': x, 'adapter_ids': adapter_ids, 'weight': weight}
    _L1_cond_all = _L1_cond_setup()
    _L1_cond_in = {k: v for k, v in _L1_cond_all.items() if k in ('weight',)}
    del _L1_cond_all

    def _L1_ffn_setup():
        import jax, jax.numpy as jnp
        import numpy as np
        BATCH, TOK, DIM, OUT = (4, 256, 512, 512)
        E, R, TOP_K = (8, 16, 2)
        SCALING = 16.0 / R
        key = jax.random.key(seed)
        ks = jax.random.split(key, 6)
        return {'x': jax.random.normal(ks[0], (BATCH, TOK, DIM), dtype=jnp.float32), 'W_base': jax.random.normal(ks[1], (OUT, DIM), dtype=jnp.float32) / np.sqrt(DIM), 'b_base': jax.random.normal(ks[2], (OUT,), dtype=jnp.float32) * 0.01, 'W_gate': jax.random.normal(ks[3], (E, DIM), dtype=jnp.float32) * 0.01, 'A': jax.random.normal(ks[4], (E, R, DIM), dtype=jnp.float32) / np.sqrt(DIM), 'B': jax.random.normal(ks[5], (OUT, OUT // OUT * R * 0 + R), dtype=jnp.float32)[None].repeat(E, 0) * 0.0 + jax.random.normal(ks[5], (E, OUT, R), dtype=jnp.float32) * 0.02}
    _L1_ffn_all = _L1_ffn_setup()
    _L1_ffn_in = {k: v for k, v in _L1_ffn_all.items() if k in ('W_base', 'b_base', 'W_gate', 'A', 'B')}
    del _L1_ffn_all
    return {'x': x, 'itok_B_0_23': itok_B_0_23, 'itok_B_0_15': itok_B_0_15, 'L0_cond_W': _L0_cond_in['W'], 'L0_cond_b': _L0_cond_in['b'], 'L0_cond_lora_As': _L0_cond_in['lora_As'], 'L0_cond_lora_Bs': _L0_cond_in['lora_Bs'], 'L0_ffn_A': _L0_ffn_in['A'], 'L0_ffn_B': _L0_ffn_in['B'], 'L0_ffn_Wr': _L0_ffn_in['Wr'], 'L1_cond_weight': _L1_cond_in['weight'], 'L1_ffn_W_base': _L1_ffn_in['W_base'], 'L1_ffn_b_base': _L1_ffn_in['b_base'], 'L1_ffn_W_gate': _L1_ffn_in['W_gate'], 'L1_ffn_A': _L1_ffn_in['A'], 'L1_ffn_B': _L1_ffn_in['B']}

def reference(x, itok_B_0_23, itok_B_0_15, L0_cond_W, L0_cond_b, L0_cond_lora_As, L0_cond_lora_Bs, L0_ffn_A, L0_ffn_B, L0_ffn_Wr, L1_cond_weight, L1_ffn_W_base, L1_ffn_b_base, L1_ffn_W_gate, L1_ffn_A, L1_ffn_B):
    import jax
    import jax.numpy as jnp

    def _L0_cond_ref(x, adapter_mapping, W, b, lora_As, lora_Bs):
        import jax, jax.numpy as jnp
        import numpy as np
        R = 16
        ALPHA = 32
        SCALING = ALPHA / R
        SLOTS = 32
        IN_F = 512
        OUT_F = 512
        B, T = (8, 128)
        base_out = jnp.einsum('bti,oi->bto', x, W) + b
        A = lora_As[adapter_mapping]
        Bm = lora_Bs[adapter_mapping]
        lora_h = jnp.einsum('bti,bir->btr', x, A)
        lora_out = jnp.einsum('btr,bro->bto', lora_h, Bm)
        return base_out + lora_out * SCALING

    def _L0_ffn_ref(x, A, B, Wr):
        import jax, jax.numpy as jnp
        import numpy as np
        LORA_R = 16
        SCALE = 16.0 / np.sqrt(16.0)
        NUM_EXPERTS = 4
        TOP_K = 2
        IN_F = 512
        OUT_F = 512
        orig_shape = x.shape
        flat = x.reshape(-1, orig_shape[-1])
        logits = flat @ Wr.T
        topk_vals, topk_idx = jax.lax.top_k(logits, TOP_K)
        T = flat.shape[0]
        neg_inf = jnp.finfo(logits.dtype).min
        sparse = jnp.full_like(logits, neg_inf)
        rows = jnp.arange(T)[:, None]
        sparse = sparse.at[rows, topk_idx].set(topk_vals)
        gates = jax.nn.softmax(sparse, axis=-1)
        mid = jnp.einsum('tf,erf->ter', flat, A)
        all_deltas = jnp.einsum('ter,eor->teo', mid, B) * SCALE
        delta = jnp.sum(gates[:, :, None] * all_deltas, axis=1)
        return delta.reshape(*orig_shape[:-1], -1)

    def _L1_cond_ref(x, adapter_ids, weight):
        import jax, jax.numpy as jnp
        import numpy as np
        MAX_LORAS = 16
        IN, OUT = (512, 512)
        B, S = (8, 256)
        w = weight[adapter_ids]
        return jnp.einsum('bsi,boi->bso', x, w)

    def _L1_ffn_ref(x, W_base, b_base, W_gate, A, B):
        import jax, jax.numpy as jnp
        import numpy as np
        BATCH, TOK, DIM, OUT = (4, 256, 512, 512)
        E, R, TOP_K = (8, 16, 2)
        SCALING = 16.0 / R
        result = jnp.einsum('bnd,od->bno', x, W_base) + b_base
        logits = jnp.einsum('bnd,ed->bne', x, W_gate)
        probs = jax.nn.softmax(logits.astype(jnp.float32), axis=-1)
        top_p, top_i = jax.lax.top_k(probs, TOP_K)
        top_p = top_p / jnp.sum(top_p, axis=-1, keepdims=True)
        top_p = top_p.astype(x.dtype)
        route_w = jnp.sum(jax.nn.one_hot(top_i, E, dtype=x.dtype) * top_p[..., None], axis=-2)
        h = jnp.einsum('bnd,erd->bner', x, A)
        hw = h * route_w[..., None]
        delta = jnp.einsum('bner,eor->bno', hw, B)
        return result + delta * SCALING
    x = x + _L0_ffn_ref(_L0_cond_ref(x, itok_B_0_23, L0_cond_W, L0_cond_b, L0_cond_lora_As, L0_cond_lora_Bs), L0_ffn_A, L0_ffn_B, L0_ffn_Wr)
    x = x + _L1_ffn_ref(_L1_cond_ref(x, itok_B_0_15, L1_cond_weight), L1_ffn_W_base, L1_ffn_b_base, L1_ffn_W_gate, L1_ffn_A, L1_ffn_B)
    return x

_drawn_inputs = setup_inputs


def setup_inputs(seed=0):
    import zlib

    import numpy as np

    out = dict(_drawn_inputs(seed))
    spreads = {}
    factors = {'L1_ffn_b_base': 6.271, 'L1_ffn_W_gate': 7.686}
    for name, (base, spread) in spreads.items():
        noise = np.random.default_rng([zlib.crc32(name.encode()), seed]).standard_normal(out[name].shape)
        drawn = base * np.exp(spread * noise) if base else spread * noise
        out[name] = jnp.asarray(drawn.astype(out[name].dtype))
    for name, factor in factors.items():
        out[name] = (out[name] * factor).astype(out[name].dtype)
    return out
```

```python
import concourse.bass as bass
from concourse import mybir
from contextlib import ExitStack


def adaln_ffn_kernel(nc, xT_dram, base0_dram, probe0_dram, bias0_dram, lora_dram, up0_dram, cond1_dram,
                     base1_dram, probe1_dram, up1_dram, bias1_dram, slot0_dram, slot1_dram,
                     consts_dram, out_dram):
    fp32 = mybir.dt.float32
    fp32r = mybir.dt.float32r
    i32 = mybir.dt.int32
    ALU = mybir.AluOpType
    ACT = mybir.ActivationFunctionType
    AX = mybir.AxisListType

    P = 128
    NB, T, D = out_dram.shape
    K = D // P
    E0 = 4
    E1 = 8
    R = 16
    Q0 = E0 + E0 * R
    Q1 = E1 + E1 * R
    HB = NB // 2
    LORA_SCALE = 2.0
    FFN0_SCALE = 4.0

    ctx = ExitStack()
    with ctx:
        def sb(name, shape, dt=fp32):
            return ctx.enter_context(nc.sbuf_tensor(name, shape, dt))

        def sem(name):
            return ctx.enter_context(nc.semaphore(name))

        xT = sb("xT", [P, NB, K, T])
        x1T = sb("x1T", [P, NB, K, T])
        base0 = sb("base0", [P, K, D])
        probe0 = sb("probe0", [P, K, Q0])
        bias0 = sb("bias0", [P, K])
        bias0_wide = sb("bias0_wide", [P, K, P])
        lora = sb("lora", [P, NB, 2, K, R])
        loraB = sb("loraB", [P, K, NB, R])
        up0 = sb("up0", [E0 * R, D])
        slots = sb("slots", [1, 2 * NB], i32)
        C_ID, C_OWN, C_LOW0, C_LOW1 = 0, P, P + NB, P + NB + E0 * E0
        consts = sb("consts", [P, C_LOW1 + E1 * E1])
        ident = consts[:, C_ID:C_ID + P]
        own = consts[:, C_OWN:C_OWN + NB]
        low0 = consts[:, C_LOW0:C_LOW0 + E0 * E0]
        low1 = consts[:, C_LOW1:C_LOW1 + E1 * E1]
        identr = sb("identr", [P, P], fp32r)
        fold0 = sb("fold0", [P, K, Q0])
        biasq = sb("biasq", [P, Q0])
        downs = sb("downs", [T, NB * R])
        downsT = sb("downsT", [NB * R, T])
        loraq = sb("loraq", [NB * R, NB, Q0])
        q0 = sb("q0", [T, NB, Q0])
        hw0 = sb("hw0", [T, NB, E0 * R])
        hw0T = sb("hw0T", [E0 * R, NB, T])

        base1f = sb("base1f", [P, K, D])
        base1h = sb("base1h", [P, K, D], fp32r)
        base1l = sb("base1l", [P, K, D], fp32r)
        probe1f = sb("probe1f", [P, K, Q1])
        probe1h = sb("probe1h", [P, K, Q1], fp32r)
        probe1l = sb("probe1l", [P, K, Q1], fp32r)
        up1f = sb("up1f", [E1 * R, D])
        up1h = sb("up1h", [E1 * R, D], fp32r)
        up1l = sb("up1l", [E1 * R, D], fp32r)
        bias1 = sb("bias1", [P, D])

        cond1f = [sb(f"cond1f{s}", [P, K, D]) for s in range(2)]
        cond1h = [sb(f"cond1h{s}", [P, K, D], fp32r) for s in range(2)]
        cond1l = [sb(f"cond1l{s}", [P, K, D], fp32r) for s in range(2)]
        x1h = [sb(f"x1h{s}", [P, K, T], fp32r) for s in range(2)]
        x1l = [sb(f"x1l{s}", [P, K, T], fp32r) for s in range(2)]
        y_sb = [sb(f"y_sb{s}", [T, D]) for s in range(2)]
        yTh = [sb(f"yTh{s}", [P, K, T], fp32r) for s in range(2)]
        yTl = [sb(f"yTl{s}", [P, K, T], fp32r) for s in range(2)]
        x1b = [sb(f"x1b{s}", [T, D]) for s in range(2)]
        hw1 = [sb(f"hw1{s}", [T, E1 * R]) for s in range(2)]
        hw1Th = [sb(f"hw1Th{s}", [E1 * R, T], fp32r) for s in range(2)]
        hw1Tl = [sb(f"hw1Tl{s}", [E1 * R, T], fp32r) for s in range(2)]
        out_sb = [sb(f"out_sb{s}", [T, D]) for s in range(2)]

        def route_tiles(tag, nb, e):
            return {n: sb(f"{n}{tag}", [T, nb] + s) for n, s in dict(
                lg=[e], top=[1], low=[e], ex=[e], gt=[e, e], eq=[e, e], eqm=[e, e], ahead=[e, e],
                rank=[e], w=[e], total=[1], inv=[1], gate=[e]).items()}
        r0 = route_tiles("_0", NB, E0)
        r1 = route_tiles("_1", 1, E1)

        bank = [ctx.enter_context(nc.psum_tensor(f"bank{i}", [P, 512], fp32)) for i in range(8)]
        fold_ps = bank[0][:, 0:K * Q0].rearrange("p (k q) -> p k q", k=K)
        biasq_ps = bank[1][:, 0:Q0]
        loraq_ps = bank[1][:, Q0:2 * Q0]
        downs_ps = bank[2][:, 0:NB * R]
        downsT_ps = bank[3][:, 0:T]
        q0_ps = [bank[5][:, 0:HB * Q0].rearrange("p (b q) -> p b q", b=HB),
                 bank[6][:, 0:HB * Q0].rearrange("p (b q) -> p b q", b=HB)]
        hw0T_ps = [bank[4], bank[0]]
        delta0_ps = [bank[7], bank[3]]
        y_ps = bank[0]
        yT_ps = bank[1]
        q1_ps = bank[2]
        hw1T_ps = bank[3]
        x1_ps = bank[4]
        out_ps = [bank[5], bank[6]]

        slots_in = sem("slots_in")
        probe0_in = sem("probe0_in")
        bias0_in = sem("bias0_in")
        base0_in = sem("base0_in")
        x_in = [sem(f"x_in{h}") for h in range(2)]
        lora_in = sem("lora_in")
        consts_in = sem("consts_in")
        up0_in = sem("up0_in")
        base1_in = sem("base1_in")
        probe1_in = sem("probe1_in")
        up1_in = sem("up1_in")
        bias1_in = sem("bias1_in")
        cond1_in = [sem(f"cond1_in{s}") for s in range(2)]
        bias_wide = sem("bias_wide")
        loraB_ready = sem("loraB_ready")
        fold_done = sem("fold_done")
        fold_ready = sem("fold_ready")
        small_done = sem("small_done")
        biasq_ready = sem("biasq_ready")
        loraq_ready = sem("loraq_ready")
        downs_done = sem("downs_done")
        downs_ready = sem("downs_ready")
        downsT_done = sem("downsT_done")
        downsT_ready = sem("downsT_ready")
        q0_done = sem("q0_done")
        low0_ready = sem("low0_ready")
        ex0_ready = sem("ex0_ready")
        route0_step = sem("route0_step")
        hw0T_done = sem("hw0T_done")
        hw0T_ready = [sem(f"hw0T_ready{h}") for h in range(2)]
        delta0_done = sem("delta0_done")
        x1T_ready = sem("x1T_ready")
        identr_ready = sem("identr_ready")
        base1_hi = sem("base1_hi")
        base1_lo = sem("base1_lo")
        cond1_hi = sem("cond1_hi")
        cond1_lo = sem("cond1_lo")
        x1_hi = sem("x1_hi")
        x1_lo = sem("x1_lo")
        y_done = sem("y_done")
        x1_done = sem("x1_done")
        y_ready = sem("y_ready")
        x1b_ready = sem("x1b_ready")
        yT_done = sem("yT_done")
        yT_hi = sem("yT_hi")
        yT_lo = sem("yT_lo")
        q1_done = sem("q1_done")
        route1_step = sem("route1_step")
        low1_ready = sem("low1_ready")
        ex1_ready = sem("ex1_ready")
        hw1_ready = sem("hw1_ready")
        hw1T_done = sem("hw1T_done")
        hw1T_hi = sem("hw1T_hi")
        hw1T_lo = sem("hw1T_lo")
        out_done = sem("out_done")
        out_ready = sem("out_ready")
        stored = [sem(f"stored{s}") for s in range(2)]

        block = ctx.enter_context(nc.Block())

        @block.sync
        def _(sp):
            sp.dma_start(slots[:, 0:NB], slot0_dram).then_inc(slots_in, 16)
            sp.dma_start(slots[:, NB:2 * NB], slot1_dram).then_inc(slots_in, 16)
            sp.dma_start(probe0[:], probe0_dram).then_inc(probe0_in, 16)
            sp.dma_start(base0[:], base0_dram).then_inc(base0_in, 16)
            sp.dma_start(xT[:, 0:HB], xT_dram[:, 0:HB]).then_inc(x_in[0], 16)
            sp.wait_ge(slots_in, 32)
            for b in range(NB):
                s = sp.value_load(slots[0:1, b:b + 1], min_val=0, max_val=lora_dram.shape[0] - 1)
                sp.dma_start(lora[:, b], lora_dram[bass.ds(s, 1)].rearrange("s p h k r -> p (s h) k r")
                             ).then_inc(lora_in, 16)
            sp.dma_start(xT[:, HB:NB], xT_dram[:, HB:NB]).then_inc(x_in[1], 16)
            sp.dma_start(up0[:], up0_dram).then_inc(up0_in, 16)

            def load_cond(b, p):
                s = sp.value_load(slots[0:1, bass.ds(NB + b, 1)], min_val=0, max_val=cond1_dram.shape[0] - 1)
                sp.dma_start(cond1f[p][:], cond1_dram[bass.ds(s, 1)].rearrange("s p k n -> p (s k) n")
                             ).then_inc(cond1_in[p], 16)

            load_cond(0, 0)
            sp.dma_start(base1f[:], base1_dram).then_inc(base1_in, 16)
            sp.dma_start(probe1f[:], probe1_dram).then_inc(probe1_in, 16)
            load_cond(1, 1)
            sp.dma_start(up1f[:], up1_dram).then_inc(up1_in, 16)
            sp.dma_start(bias1[:], bias1_dram.to_broadcast([P, D])).then_inc(bias1_in, 16)
            with sp.Fori(1, NB // 2) as j:
                for p in range(2):
                    sp.wait_ge(cond1_hi, 2 * (2 * j + p - 1))
                    sp.wait_ge(cond1_lo, 2 * (2 * j + p - 1))
                    load_cond(2 * j + p, p)

        @block.gpsimd
        def _(pool):
            for i, (lo, full, hi) in enumerate([(probe1l, probe1f, probe1h), (base1l, base1f, base1h),
                                                (up1l, up1f, up1h)]):
                pool.wait_ge(base1_hi, i + 1)
                nc.gpsimd.tensor_tensor(lo[:], full[:], hi[:].bitcast(fp32), ALU.subtract).then_inc(base1_lo, 1)

        @block.scalar
        def _(act):
            for p in range(2):
                act.sem_inc(stored[p], 16)
            act.dma_start(consts[:], consts_dram).then_inc(consts_in, 16)
            act.dma_start(bias0[:], bias0_dram).then_inc(bias0_in, 16)
            act.wait_ge(consts_in, 16)
            nc.scalar.copy(identr[:], ident).then_inc(identr_ready, 1)
            act.wait_ge(fold_done, 1)
            nc.scalar.copy(fold0[:], fold_ps).then_inc(fold_ready, 1)
            act.wait_ge(downs_done, 1)
            nc.scalar.copy(downs[:], downs_ps).then_inc(downs_ready, 1)
            act.wait_ge(downsT_done, 1)
            nc.scalar.copy(downsT[:], downsT_ps).then_inc(downsT_ready, 1)

            def cond_hi(j, p, half):
                b = 2 * j + p
                if half == 0:
                    act.wait_ge(cond1_in[p], 16 * (j + 1))
                    if not (isinstance(b, int) and b < 2):
                        act.wait_ge(y_done, b - 1)
                ks = slice(half * K // 2, (half + 1) * K // 2)
                nc.scalar.copy(cond1h[p][:, ks], cond1f[p][:, ks]).then_inc(cond1_hi, 1)

            def x_hi(j, p):
                b = 2 * j + p
                if isinstance(b, int) and b < 2:
                    act.wait_ge(x1T_ready, 2)
                else:
                    act.wait_ge(x1T_ready, NB)
                    act.wait_ge(x1_done, b - 1)
                nc.scalar.copy(x1h[p][:], x1T[:, bass.ds(b, 1)].rearrange("p b k t -> p (b k) t")
                               ).then_inc(x1_hi, 1)

            cond_hi(0, 0, 0)
            cond_hi(0, 0, 1)
            act.wait_ge(low0_ready, 1)
            nc.scalar.activation(r0["ex"][:], r0["low"][:], ACT.Exp).then_inc(ex0_ready, 1)
            act.wait_ge(probe1_in, 16)
            nc.scalar.copy(probe1h[:], probe1f[:]).then_inc(base1_hi, 1)
            act.wait_ge(hw0T_done, 1)
            nc.scalar.copy(hw0T[:, 0:HB], hw0T_ps[0][0:E0 * R, :].rearrange("p (b t) -> p b t", b=HB)
                           ).then_inc(hw0T_ready[0], 1)
            act.wait_ge(base1_in, 16)
            nc.scalar.copy(base1h[:], base1f[:]).then_inc(base1_hi, 1)
            x_hi(0, 0)
            cond_hi(0, 1, 0)
            cond_hi(0, 1, 1)
            x_hi(0, 1)
            act.wait_ge(up1_in, 16)
            nc.scalar.copy(up1h[:], up1f[:]).then_inc(base1_hi, 1)

            def y_copy(b, p):
                act.wait_ge(y_done, b + 1)
                if not (isinstance(b, int) and b < 2):
                    act.wait_ge(yT_done, b - 1)
                nc.scalar.copy(y_sb[p][:], y_ps[:]).then_inc(y_ready, 1)

            def step(j, p, first=False, last=False, split=True):
                b = 2 * j + p
                jn, pn = (j, 1) if p == 0 else (j + 1, 0)
                act.wait_ge(yT_done, b + 1)
                nc.scalar.copy(yTh[p][:], yT_ps[:].rearrange("p (k t) -> p k t", k=K)).then_inc(yT_hi, 1)
                if not first:
                    hwT_hi(b - 1, 1 - p)
                if split:
                    cond_hi(j + 1, p, 0)
                if not last:
                    y_copy(b + 1, pn)
                if split:
                    x_hi(j + 1, p)
                act.wait_ge(low1_ready, b + 1)
                nc.scalar.activation(r1["ex"][:], r1["low"][:], ACT.Exp).then_inc(ex1_ready, 1)
                if not first:
                    store(b - 1, 1 - p)
                if split:
                    cond_hi(j + 1, p, 1)

            def hwT_hi(b, p):
                act.wait_ge(hw1T_done, b + 1)
                nc.scalar.copy(hw1Th[p][:], hw1T_ps[:, 0:T]).then_inc(hw1T_hi, 1)

            def store(b, p):
                act.wait_ge(out_ready, b + 1)
                act.dma_start(out_dram[bass.ds(b, 1)].rearrange("b t n -> t (b n)"), out_sb[p][:]
                              ).then_inc(stored[p], 16)

            y_copy(0, 0)
            step(0, 0, first=True)
            step(0, 1)
            with act.Fori(1, NB // 2 - 1) as j:
                step(j, 0)
                step(j, 1)
            step(NB // 2 - 1, 0, split=False)
            step(NB // 2 - 1, 1, split=False, last=True)
            hwT_hi(NB - 1, 1)
            store(NB - 1, 1)
            for p in range(2):
                act.wait_ge(stored[p], 16 * (NB // 2 + 1))

        @block.vector
        def _(dve):
            TT = nc.vector.tensor_tensor
            dve.wait_ge(bias0_in, 16)
            nc.vector.tensor_copy(bias0_wide[:], bias0[:].rearrange("p (k a) -> p k a", a=1).to_broadcast([P, K, P])
                                  ).then_inc(bias_wide, 1)
            dve.wait_ge(lora_in, 16 * NB)
            nc.vector.tensor_copy(loraB[:], lora[:, :, 1].rearrange("p b k r -> p k b r")).then_inc(loraB_ready, 1)
            dve.wait_ge(small_done, 1)
            nc.vector.tensor_copy(biasq[:], biasq_ps).then_inc(biasq_ready, 1)
            dve.wait_ge(consts_in, 16)
            nc.vector.scalar_tensor_tensor(
                loraq[:], loraq_ps.rearrange("p (a q) -> p a q", a=1).to_broadcast([P, NB, Q0]), LORA_SCALE,
                own.rearrange("p (b a) -> p b a", a=1).to_broadcast([P, NB, Q0]),
                ALU.mult, ALU.mult).then_inc(loraq_ready, 1)
            dve.wait_ge(q0_done, 1)
            dve.wait_ge(biasq_ready, 1)
            for h in range(2):
                TT(q0[:, h * HB:(h + 1) * HB], q0_ps[h],
                   biasq[:].rearrange("p (a q) -> p a q", a=1).to_broadcast([P, HB, Q0]),
                   ALU.add).then_inc(route0_step, 1)

            def route(r, logits, nb, e, low, chain, at, low_ready, ex_ready, b):
                def after(n):
                    dve.wait_ge(chain, at + n)

                lj = logits.rearrange("p b (a j) -> p b a j", a=1).to_broadcast([T, nb, e, e])
                le = logits.rearrange("p b (e a) -> p b e a", a=1).to_broadcast([T, nb, e, e])
                if nb == 1:
                    pairs = "p b e j -> p (b e) j"
                    lowm = low.rearrange("p (e j) -> p e j", j=e)
                    nar = lambda t: t.rearrange(pairs)
                else:
                    lowm = low.rearrange("p (a m) -> p a m", a=1).to_broadcast([T, nb, e * e])
                    nar = lambda t: t.rearrange("p b e j -> p b (e j)")
                after(0)
                nc.vector.reduce_max(r["top"][:].rearrange("p b a -> p (b a)"), logits, AX.X).then_inc(chain, 1)
                TT(r["gt"][:], lj, le, ALU.is_gt).then_inc(chain, 1)
                TT(r["eq"][:], lj, le, ALU.is_equal).then_inc(chain, 1)
                after(1)
                TT(r["low"][:], logits, r["top"][:].to_broadcast([T, nb, e]), ALU.subtract).then_inc(low_ready, 1)
                after(3)
                TT(nar(r["eqm"][:]), nar(r["eq"][:]), lowm, ALU.mult).then_inc(chain, 1)
                after(4)
                TT(r["ahead"][:], r["gt"][:], r["eqm"][:], ALU.add).then_inc(chain, 1)
                after(5)
                nc.vector.reduce_sum(r["rank"][:].rearrange("p b e -> p (b e)"),
                                     r["ahead"][:].rearrange("p b e j -> p (b e) j"), AX.X).then_inc(chain, 1)
                after(6)
                dve.wait_ge(ex_ready, b + 1)
                nc.vector.scalar_tensor_tensor(r["w"][:], r["rank"][:], 2.0, r["ex"][:], ALU.is_lt, ALU.mult
                                               ).then_inc(chain, 1)
                after(7)
                nc.vector.reduce_sum(r["total"][:].rearrange("p b a -> p (b a)"), r["w"][:], AX.X).then_inc(chain, 1)
                after(8)
                nc.vector.reciprocal(r["inv"][:], r["total"][:]).then_inc(chain, 1)
                after(9)

            route(r0, q0[:, :, 0:E0], NB, E0, low0, route0_step, 2, low0_ready, ex0_ready, 0)
            nc.vector.scalar_tensor_tensor(r0["gate"][:], r0["w"][:], FFN0_SCALE, r0["inv"][:].to_broadcast([T, NB, E0]),
                                           ALU.mult, ALU.mult).then_inc(route0_step, 1)
            dve.wait_ge(route0_step, 12)
            for h in range(2):
                hb = slice(h * HB, (h + 1) * HB)
                TT(hw0[:, hb].rearrange("p b (e r) -> p b e r", r=R),
                   q0[:, hb, E0:Q0].rearrange("p b (e r) -> p b e r", r=R),
                   r0["gate"][:, hb].rearrange("p b (e a) -> p b e a", a=1).to_broadcast([T, HB, E0, R]),
                   ALU.mult).then_inc(route0_step, 1)

            def cond_lo(b, p, half):
                dve.wait_ge(cond1_hi, 2 * b + half + 1)
                if half == 0 and not (isinstance(b, int) and b < 2):
                    dve.wait_ge(y_done, b - 1)
                ks = slice(half * K // 2, (half + 1) * K // 2)
                TT(cond1l[p][:, ks], cond1f[p][:, ks], cond1h[p][:, ks].bitcast(fp32), ALU.subtract
                   ).then_inc(cond1_lo, 1)

            def x_lo(b, p):
                dve.wait_ge(x1_hi, b + 1)
                TT(x1l[p][:], x1T[:, bass.ds(b, 1)].rearrange("p b k t -> p (b k) t"), x1h[p][:].bitcast(fp32),
                   ALU.subtract).then_inc(x1_lo, 1)

            def x1_pair(j):
                for c in range(2):
                    dve.wait_ge(delta0_done, 2 * j + c + 1)
                    at = lambda t: t[:, 2 * j:2 * j + 2, 2 * c:2 * c + 2].rearrange("p b k t -> p k b t")
                    TT(at(x1T), delta0_ps[c][:].rearrange("p (k b t) -> p k b t", k=2, b=2), at(xT),
                       ALU.add).then_inc(x1T_ready, 1)

            cond_lo(0, 0, 0)
            cond_lo(0, 0, 1)
            dve.wait_ge(hw0T_done, 2)
            nc.vector.tensor_copy(hw0T[:, HB:NB], hw0T_ps[1][0:E0 * R, :].rearrange("p (b t) -> p b t", b=HB)
                                  ).then_inc(hw0T_ready[1], 1)
            x1_pair(0)
            x_lo(0, 0)
            cond_lo(1, 1, 0)
            x1_pair(1)
            cond_lo(1, 1, 1)
            x_lo(1, 1)
            x1_pair(2)
            x1_pair(3)

            def x1_bias(b, p):
                dve.wait_ge(x1_done, b + 1)
                if not (isinstance(b, int) and b < 2):
                    dve.wait_ge(out_ready, b - 1)
                TT(x1b[p][:], x1_ps[:], bias1[:], ALU.add).then_inc(x1b_ready, 1)

            def hwT_lo(b, p):
                dve.wait_ge(hw1T_hi, b + 1)
                TT(hw1Tl[p][:], hw1T_ps[:, 0:T], hw1Th[p][:].bitcast(fp32), ALU.subtract).then_inc(hw1T_lo, 1)

            def finish(j, p):
                b = 2 * j + p
                dve.wait_ge(out_done, b + 1)
                dve.wait_ge(x1b_ready, b + 1)
                dve.wait_ge(stored[p], 16 * (j + 1))
                TT(out_sb[p][:], out_ps[p][:], x1b[p][:], ALU.add).then_inc(out_ready, 1)

            ROUTE1 = 10

            def step(j, p, first=False, last=False, split=True):
                b = 2 * j + p
                pn = 1 - p
                dve.wait_ge(yT_hi, b + 1)
                TT(yTl[p][:], yT_ps[:].rearrange("p (k t) -> p k t", k=K), yTh[p][:].bitcast(fp32), ALU.subtract
                   ).then_inc(yT_lo, 1)
                if not first:
                    hwT_lo(b - 1, pn)
                if split:
                    cond_lo(b + 2, p, 0)
                if not first:
                    finish(j if p else j - 1, pn)
                if not last:
                    x1_bias(b + 1, pn)
                dve.wait_ge(q1_done, b + 1)
                nc.vector.tensor_copy(r1["lg"][:, 0], q1_ps[:, 0:E1]).then_inc(route1_step, 1)
                route(r1, r1["lg"][:], 1, E1, low1, route1_step, ROUTE1 * b + 1, low1_ready, ex1_ready, b)
                if not (isinstance(b, int) and b < 2):
                    dve.wait_ge(hw1T_done, b - 1)
                nc.vector.scalar_tensor_tensor(
                    hw1[p][:].rearrange("p (e r) -> p e r", r=R),
                    q1_ps[:, E1:Q1].rearrange("p (e r) -> p e r", r=R), r1["inv"][:, 0],
                    r1["w"][:].rearrange("p a e -> p e a").to_broadcast([T, E1, R]), ALU.mult, ALU.mult
                    ).then_inc(hw1_ready, 1)
                if split:
                    x_lo(b + 2, p)
                    cond_lo(b + 2, p, 1)

            dve.wait_ge(bias1_in, 16)
            x1_bias(0, 0)
            step(0, 0, first=True)
            step(0, 1)
            with dve.Fori(1, NB // 2 - 1) as j:
                step(j, 0)
                step(j, 1)
            step(NB // 2 - 1, 0, split=False)
            step(NB // 2 - 1, 1, split=False, last=True)
            hwT_lo(NB - 1, 1)
            finish(NB // 2 - 1, 1)

        @block.tensor
        def _(pe):
            mm = nc.tensor.matmul
            pe.wait_ge(probe0_in, 16)
            pe.wait_ge(base0_in, 16)
            for c in range(K):
                for k in range(K):
                    last = mm(fold_ps[:, c], base0[:, k, c * P:(c + 1) * P], probe0[:, k], start=k == 0, stop=k == K - 1)
            last.then_inc(fold_done, 1)
            pe.wait_ge(bias_wide, 1)
            for k in range(K):
                mm(biasq_ps, bias0_wide[:, k], probe0[:, k], start=k == 0, stop=k == K - 1)
            pe.wait_ge(loraB_ready, 1)
            for k in range(K):
                last = mm(loraq_ps, loraB[:, k].rearrange("p b r -> p (b r)"), probe0[:, k],
                          start=k == 0, stop=k == K - 1)
            last.then_inc(small_done, 1)
            for b in range(NB):
                if b % HB == 0:
                    pe.wait_ge(x_in[b // HB], 16)
                for k in range(K):
                    last = mm(downs_ps[:, b * R:(b + 1) * R], xT[:, b, k], lora[:, b, 0, k],
                              start=k == 0, stop=k == K - 1)
            last.then_inc(downs_done, 1)
            pe.wait_ge(fold_ready, 1)
            for b in range(NB):
                for k in range(K):
                    mm(q0_ps[b // HB][:, b % HB], xT[:, b, k], fold0[:, k], start=b % HB == 0 and k == 0, stop=False,
                       skip_group_check=True)
                if b == 1:
                    pe.wait_ge(consts_in, 16)
                    pe.wait_ge(downs_ready, 1)
                    nc.tensor.transpose(downsT_ps, downs[:], ident).then_inc(downsT_done, 1)
            pe.wait_ge(downsT_ready, 1)
            pe.wait_ge(loraq_ready, 1)
            for h in range(2):
                last = mm(q0_ps[h], downsT[:], loraq[:, h * HB:(h + 1) * HB], start=False, stop=True,
                          skip_group_check=True)
            last.then_inc(q0_done, 1)
            for h in range(2):
                pe.wait_ge(route0_step, 13 + h)
                for b in range(HB):
                    last = nc.tensor.transpose(hw0T_ps[h][0:E0 * R, b * T:(b + 1) * T], hw0[:, h * HB + b], ident)
                last.then_inc(hw0T_done, 1)
            pe.wait_ge(up0_in, 16)

            def delta0(j):
                pe.wait_ge(hw0T_ready[j // 2], 1)
                for k in range(K):
                    if j > 0 and k % 2 == 0:
                        pe.wait_ge(x1T_ready, 2 * (j - 1) + k // 2 + 1)
                    last = mm(delta0_ps[k // 2][:, k % 2 * 2 * T:(k % 2 + 1) * 2 * T], up0[:, k * P:(k + 1) * P],
                              hw0T[:, 2 * j:2 * j + 2], start=True, stop=True)
                    if k % 2:
                        last.then_inc(delta0_done, 1)

            def y_product(b, p, half):
                if half == 0:
                    pe.wait_ge(x1_lo, b + 1)
                    if not (isinstance(b, int) and b < 1):
                        pe.wait_ge(y_ready, b)
                        pe.wait_ge(x1b_ready, b)
                pe.wait_ge(cond1_lo, 2 * b + half + 1)
                for k in range(half * K // 2, (half + 1) * K // 2):
                    mm(y_ps[:], x1h[p][:, k], cond1h[p][:, k], start=k == 0, stop=False)
                    mm(y_ps[:], x1h[p][:, k], cond1l[p][:, k], start=False, stop=False)
                    last = mm(y_ps[:], x1l[p][:, k], cond1h[p][:, k], start=False, stop=k == K - 1)
                    if k == K - 1:
                        last.then_inc(y_done, 1)
                    mm(x1_ps[:, k * P:(k + 1) * P], x1h[p][:, k], identr[:], start=True, stop=False)
                    last = mm(x1_ps[:, k * P:(k + 1) * P], x1l[p][:, k], identr[:], start=False, stop=True)
                    if k == K - 1:
                        last.then_inc(x1_done, 1)

            def hw_transpose(b, p):
                pe.wait_ge(hw1_ready, b + 1)
                if not (isinstance(b, int) and b < 1):
                    pe.wait_ge(hw1T_lo, b)
                nc.tensor.transpose(hw1T_ps[:, 0:T], hw1[p][:], ident).then_inc(hw1T_done, 1)

            def low_rank(b, p):
                pe.wait_ge(hw1T_lo, b + 1)
                mm(out_ps[p][:], hw1Th[p][:], up1h[:], start=False, stop=False)
                mm(out_ps[p][:], hw1Th[p][:], up1l[:], start=False, stop=False)
                mm(out_ps[p][:], hw1Tl[p][:], up1h[:], start=False, stop=True).then_inc(out_done, 1)

            def step(j, p, first=False, last=False):
                b = 2 * j + p
                pn = 1 - p
                if not last:
                    y_product(b + 1, pn, 0)
                pe.wait_ge(y_ready, b + 1)
                if not first:
                    pe.wait_ge(yT_lo, b)
                for k in range(K):
                    m = nc.tensor.transpose(yT_ps[:, k * T:(k + 1) * T], y_sb[p][:, k * P:(k + 1) * P], ident)
                m.then_inc(yT_done, 1)
                if not first:
                    hw_transpose(b - 1, pn)
                if not last:
                    y_product(b + 1, pn, 1)
                if not first:
                    low_rank(b - 1, pn)
                pe.wait_ge(yT_lo, b + 1)
                if not first:
                    pe.wait_ge(hw1_ready, b)
                for k in range(K):
                    mm(q1_ps[:, 0:Q1], yTh[p][:, k], probe1h[:, k], start=k == 0, stop=False)
                    mm(q1_ps[:, 0:Q1], yTh[p][:, k], probe1l[:, k], start=False, stop=False)
                    m = mm(q1_ps[:, 0:Q1], yTl[p][:, k], probe1h[:, k], start=False, stop=k == K - 1)
                m.then_inc(q1_done, 1)
                if not (isinstance(b, int) and b < 2):
                    pe.wait_ge(out_ready, b - 1)
                for k in range(K):
                    mm(out_ps[p][:], yTh[p][:, k], base1h[:, k], start=k == 0, stop=False)
                    mm(out_ps[p][:], yTh[p][:, k], base1l[:, k], start=False, stop=False)
                    mm(out_ps[p][:], yTl[p][:, k], base1h[:, k], start=False, stop=False)

            delta0(0)
            pe.wait_ge(identr_ready, 1)
            y_product(0, 0, 0)
            y_product(0, 0, 1)
            for j in range(1, NB // 2):
                delta0(j)
            pe.wait_ge(base1_lo, 3)
            step(0, 0, first=True)
            step(0, 1)
            with pe.Fori(1, NB // 2 - 1) as j:
                step(j, 0)
                step(j, 1)
            step(NB // 2 - 1, 0)
            step(NB // 2 - 1, 1, last=True)
            hw_transpose(NB - 1, 1)
            low_rank(NB - 1, 1)


def kernel(x, itok_B_0_23, itok_B_0_15, L0_cond_W, L0_cond_b, L0_cond_lora_As, L0_cond_lora_Bs, L0_ffn_A, L0_ffn_B,
           L0_ffn_Wr, L1_cond_weight, L1_ffn_W_base, L1_ffn_b_base, L1_ffn_W_gate, L1_ffn_A, L1_ffn_B):
    import numpy as np
    import concourse.bacc as bacc
    from concourse import mybir
    from concourse.bass_utils import run_bass_kernel_spmd

    P = 128

    def rows(a):
        a = np.asarray(a)
        n, d = a.shape
        return np.ascontiguousarray(a.T.reshape(d // P, P, n).transpose(1, 0, 2))

    x = np.asarray(x)
    NB, T, D = x.shape
    K = D // P
    W = np.asarray(L0_cond_W)
    As, Bs = np.asarray(L0_cond_lora_As), np.asarray(L0_cond_lora_Bs)
    S, _, R = As.shape
    A0, B0, Wr = np.asarray(L0_ffn_A), np.asarray(L0_ffn_B), np.asarray(L0_ffn_Wr)
    A1, B1, Wg = np.asarray(L1_ffn_A), np.asarray(L1_ffn_B), np.asarray(L1_ffn_W_gate)
    V = np.asarray(L1_cond_weight)
    E0, E1 = Wr.shape[0], Wg.shape[0]

    def lower(e):
        return np.tile(np.tril(np.ones((e, e), np.float32), -1).reshape(1, e * e), (P, 1))

    arrays = {
        "xT": x.reshape(NB, T, K, P).transpose(3, 0, 2, 1),
        "base0": W.reshape(K, P, D).transpose(1, 0, 2),
        "probe0": rows(np.concatenate([Wr, A0.reshape(E0 * R, D)])),
        "bias0": np.asarray(L0_cond_b).reshape(K, P).T,
        "lora": np.stack([As.reshape(S, K, P, R).transpose(0, 2, 1, 3), Bs.reshape(S, R, K, P).transpose(0, 3, 2, 1)], 2),
        "up0": B0.transpose(0, 2, 1).reshape(E0 * R, D),
        "cond1": V.transpose(0, 2, 1).reshape(V.shape[0], K, P, D).transpose(0, 2, 1, 3),
        "base1": rows(L1_ffn_W_base),
        "probe1": rows(np.concatenate([Wg, A1.reshape(E1 * R, D)])),
        "up1": B1.transpose(0, 2, 1).reshape(E1 * R, D),
        "bias1": np.asarray(L1_ffn_b_base).reshape(1, D),
        "slot0": np.asarray(itok_B_0_23).reshape(1, NB),
        "slot1": np.asarray(itok_B_0_15).reshape(1, NB),
        "consts": np.concatenate([np.eye(P, dtype=np.float32),
                                  np.repeat(np.eye(NB, dtype=np.float32), P // NB, axis=0),
                                  lower(E0), lower(E1)], 1),
    }
    nc = bacc.Bacc("TRN2", target_bir_lowering=False, num_devices=1)
    ins, args = {}, []
    for name, a in arrays.items():
        a = np.ascontiguousarray(a)
        ins[f"{name}_dram"] = a
        args.append(nc.dram_tensor(f"{name}_dram", a.shape, mybir.dt.from_np(a.dtype), kind="ExternalInput").ap())
    args.append(nc.dram_tensor("out_dram", (NB, T, D), mybir.dt.float32, kind="ExternalOutput").ap())
    adaln_ffn_kernel(nc, *args)
    r = run_bass_kernel_spmd(nc, [ins], core_ids=[0])
    return r.results[0]["out_dram"]
```

```python
import concourse.bass as bass
from concourse import mybir
from contextlib import ExitStack


def adaln_ffn_kernel(nc, xT_dram, base0_dram, probe0_dram, bias0_dram, lora_dram, up0_dram, cond1_dram,
                     mix1_dram, up1_dram, bias1_dram, slot0_dram, slot1_dram,
                     consts_dram, out_dram):
    fp32 = mybir.dt.float32
    fp32r = mybir.dt.float32r
    i32 = mybir.dt.int32
    ALU = mybir.AluOpType
    ACT = mybir.ActivationFunctionType
    AX = mybir.AxisListType

    P = 128
    NB, T, D = out_dram.shape
    K = D // P
    E0 = 4
    E1 = 8
    R = 16
    Q0 = E0 + E0 * R
    Q1 = E1 + E1 * R
    M1 = Q1 + D
    CA = M1 // 2
    OA = CA - Q1
    LR = P - 2 * R
    NP = NB // 2
    HB = NB // 2
    LORA_SCALE = 2.0
    FFN0_SCALE = 4.0

    ctx = ExitStack()
    with ctx:
        def sb(name, shape, dt=fp32):
            return ctx.enter_context(nc.sbuf_tensor(name, shape, dt))

        def sem(name):
            return ctx.enter_context(nc.semaphore(name))

        xT = sb("xT", [P, NB, K, T])
        x1T = sb("x1T", [P, NB, K, T])
        base0 = sb("base0", [P, K, D])
        probe0 = sb("probe0", [P, K, Q0])
        bias0 = sb("bias0", [P, K])
        lora = sb("lora", [P, NB, 2, K, R])
        loraB = sb("loraB", [P, K, NB, R])
        up0 = sb("up0", [E0 * R, D])
        slots = sb("slots", [1, 2 * NB], i32)
        C_ID, C_OWN, C_LOW0 = 0, P, P + 2
        C_LOW1 = C_LOW0 + E0 * E0
        C_EYE = C_LOW1 + E1 * E1
        consts = sb("consts", [P, C_EYE + Q0])
        ident = consts[:, C_ID:C_ID + P]
        own = consts[:, C_OWN:C_OWN + 2]
        low0 = consts[:, C_LOW0:C_LOW0 + E0 * E0]
        low1 = consts[:, C_LOW1:C_LOW1 + E1 * E1]
        eye0 = consts[:, C_EYE:C_EYE + Q0]
        foldT = sb("foldT", [Q0, D])
        bcol = sb("bcol", [P, 1])
        left0 = sb("left0", [P, NP, K, P])
        right0 = sb("right0", [P, NP, Q0])
        q0T = sb("q0T", [P, NP, 2, T])
        hw0 = sb("hw0", [T, NB, E0 * R])
        hw0T = sb("hw0T", [E0 * R, NB, T])

        mix1f = sb("mix1f", [P, K, M1])
        mix1h = sb("mix1h", [P, K, M1], fp32r)
        mix1l = sb("mix1l", [P, K, M1], fp32r)
        up1f = sb("up1f", [E1 * R, D])
        up1h = sb("up1h", [E1 * R, D], fp32r)
        up1l = sb("up1l", [E1 * R, D], fp32r)
        bias1 = sb("bias1", [P, D])

        cond1f = [sb(f"cond1f{s}", [P, K, D]) for s in range(2)]
        cond1h = [sb(f"cond1h{s}", [P, K, D], fp32r) for s in range(2)]
        cond1l = [sb(f"cond1l{s}", [P, K, D], fp32r) for s in range(2)]
        x1h = [sb(f"x1h{s}", [P, K, T], fp32r) for s in range(2)]
        x1l = [sb(f"x1l{s}", [P, K, T], fp32r) for s in range(2)]
        y_sb = [sb(f"y_sb{s}", [T, D]) for s in range(2)]
        yTh = [sb(f"yTh{s}", [P, K, T], fp32r) for s in range(2)]
        yTl = [sb(f"yTl{s}", [P, K, T], fp32r) for s in range(2)]
        x1n = sb("x1n", [T, NB, D])
        hw1 = [sb(f"hw1{s}", [T, E1 * R]) for s in range(2)]
        hw1Th = [sb(f"hw1Th{s}", [E1 * R, T], fp32r) for s in range(2)]
        hw1Tl = [sb(f"hw1Tl{s}", [E1 * R, T], fp32r) for s in range(2)]
        out_sb = [sb(f"out_sb{s}", [T, D]) for s in range(2)]

        def route_tiles(tag, nb, e):
            return {n: sb(f"{n}{tag}", [T, nb] + s) for n, s in dict(
                lg=[e], top=[1], low=[e], ex=[e], gt=[e, e], eq=[e, e], eqm=[e, e], ahead=[e, e],
                rank=[e], w=[e], total=[1], inv=[1], gate=[e]).items()}
        r0 = [route_tiles(f"_0{h}", HB, E0) for h in range(2)]
        r1 = route_tiles("_1", 1, E1)

        bank = [ctx.enter_context(nc.psum_tensor(f"bank{i}", [P, 512], fp32)) for i in range(8)]
        foldT_ps = bank[0][0:Q0, :]
        fold_ps = bank[1][:, 0:K * Q0].rearrange("p (k q) -> p k q", k=K)
        loraq_ps = bank[6][:, 0:Q0]
        bcol_ps = bank[6][0:Q0, Q0:Q0 + 1]
        q0T_ps = [bank[i][:, 0:2 * T] for i in (2, 3, 4, 7)]
        q0_ps = [bank[i][:, 0:HB * Q0].rearrange("p (b q) -> p b q", b=HB) for i in (5, 6)]
        hw0T_ps = [bank[1], bank[0]]
        delta0_ps = [bank[2], bank[3]]
        x1n_ps = [bank[4], bank[7]]
        y_ps = bank[0]
        yT_ps = bank[1]
        hw1T_ps = bank[2]
        outA_ps = [bank[5][:, 0:CA], bank[6][:, 0:CA]]
        outB_ps = [bank[4][:, 0:CA], bank[7][:, 0:CA]]

        slots_in = sem("slots_in")
        probe0_in = sem("probe0_in")
        bias0_in = sem("bias0_in")
        base0_in = [sem(f"base0_in{k}") for k in range(K)]
        x_in = [sem(f"x_in{j}") for j in range(NP)]
        lora_in = sem("lora_in")
        consts_in = sem("consts_in")
        up0_in = sem("up0_in")
        mix1_in = sem("mix1_in")
        up1_in = sem("up1_in")
        bias1_in = sem("bias1_in")
        cond1_in = [sem(f"cond1_in{s}") for s in range(2)]
        pad_zero = sem("pad_zero")
        loraB_ready = sem("loraB_ready")
        foldT_done = sem("foldT_done")
        foldT_ready = sem("foldT_ready")
        fold_done = sem("fold_done")
        left0_ready = sem("left0_ready")
        bcol_zero = sem("bcol_zero")
        bcol_ready = sem("bcol_ready")
        loraq_done = sem("loraq_done")
        right0_ready = sem("right0_ready")
        q0T_done = sem("q0T_done")
        q0T_ready = sem("q0T_ready")
        q0_done = sem("q0_done")
        low0_ready = sem("low0_ready")
        ex0_ready = sem("ex0_ready")
        route0_step = sem("route0_step")
        hw0_ready = sem("hw0_ready")
        hw0T_done = sem("hw0T_done")
        hw0T_ready = sem("hw0T_ready")
        delta0_done = sem("delta0_done")
        x1T_ready = sem("x1T_ready")
        x1n_done = sem("x1n_done")
        x1n_ready = sem("x1n_ready")
        x1b_ready = sem("x1b_ready")
        const1_hi = sem("const1_hi")
        mix1_lo = sem("mix1_lo")
        up1_lo = sem("up1_lo")
        cond1_hi = sem("cond1_hi")
        cond1_lo = sem("cond1_lo")
        x1_hi = sem("x1_hi")
        x1_lo = sem("x1_lo")
        y_done = sem("y_done")
        y_ready = sem("y_ready")
        yT_done = sem("yT_done")
        yT_hi = sem("yT_hi")
        yT_lo = sem("yT_lo")
        q1_done = sem("q1_done")
        route1_step = sem("route1_step")
        low1_ready = sem("low1_ready")
        ex1_ready = sem("ex1_ready")
        hw1_ready = sem("hw1_ready")
        hw1T_done = sem("hw1T_done")
        hw1T_hi = sem("hw1T_hi")
        hw1T_lo = sem("hw1T_lo")
        out_done = sem("out_done")
        out_ready = sem("out_ready")
        stored = [sem(f"stored{s}") for s in range(2)]

        block = ctx.enter_context(nc.Block())

        @block.sync
        def _(sp):
            sp.dma_start(slots[:, 0:NB], slot0_dram).then_inc(slots_in, 16)
            sp.dma_start(slots[:, NB:2 * NB], slot1_dram).then_inc(slots_in, 16)
            sp.dma_start(probe0[:], probe0_dram).then_inc(probe0_in, 16)
            for k in range(K):
                sp.dma_start(base0[:, k], base0_dram[:, k]).then_inc(base0_in[k], 16)
            sp.wait_ge(slots_in, 32)
            for b in range(NB):
                s = sp.value_load(slots[0:1, b:b + 1], min_val=0, max_val=lora_dram.shape[0] - 1)
                sp.dma_start(lora[:, b], lora_dram[bass.ds(s, 1)].rearrange("s p h k r -> p (s h) k r")
                             ).then_inc(lora_in, 16)
            for j in range(NP):
                sp.dma_start(xT[:, 2 * j:2 * j + 2], xT_dram[:, 2 * j:2 * j + 2]).then_inc(x_in[j], 16)
            sp.dma_start(up0[:], up0_dram).then_inc(up0_in, 16)

            def load_cond(b, p):
                s = sp.value_load(slots[0:1, bass.ds(NB + b, 1)], min_val=0, max_val=cond1_dram.shape[0] - 1)
                sp.dma_start(cond1f[p][:], cond1_dram[bass.ds(s, 1)].rearrange("s p k n -> p (s k) n")
                             ).then_inc(cond1_in[p], 16)

            load_cond(0, 0)
            sp.dma_start(mix1f[:], mix1_dram).then_inc(mix1_in, 16)
            load_cond(1, 1)
            sp.dma_start(up1f[:], up1_dram).then_inc(up1_in, 16)
            sp.dma_start(bias1[:], bias1_dram.to_broadcast([P, D])).then_inc(bias1_in, 16)
            with sp.Fori(1, NB // 2) as j:
                for p in range(2):
                    sp.wait_ge(cond1_hi, 2 * (2 * j + p - 1))
                    sp.wait_ge(cond1_lo, 2 * (2 * j + p - 1))
                    load_cond(2 * j + p, p)

        @block.gpsimd
        def _(pool):
            nc.gpsimd.memset(left0[:, :, :, Q0:LR], 0.0).then_inc(pad_zero, 1)

            def x_lo(b, p):
                pool.wait_ge(x1_hi, b + 1)
                nc.gpsimd.tensor_tensor(x1l[p][:], x1T[:, bass.ds(b, 1)].rearrange("p b k t -> p (b k) t"),
                                        x1h[p][:].bitcast(fp32), ALU.subtract).then_inc(x1_lo, 1)

            def x1_bias(b):
                pool.wait_ge(x1n_ready, b + 1)
                nc.gpsimd.tensor_tensor(x1n[:, bass.ds(b, 1)].rearrange("p b n -> p (b n)"),
                                        x1n[:, bass.ds(b, 1)].rearrange("p b n -> p (b n)"),
                                        bias1[:], ALU.add).then_inc(x1b_ready, 1)

            pool.wait_ge(const1_hi, 1)
            nc.gpsimd.tensor_tensor(mix1l[:, 0:K // 2], mix1f[:, 0:K // 2], mix1h[:, 0:K // 2].bitcast(fp32),
                                    ALU.subtract).then_inc(mix1_lo, 1)
            pool.wait_ge(const1_hi, 3)
            nc.gpsimd.tensor_tensor(up1l[:], up1f[:], up1h[:].bitcast(fp32), ALU.subtract).then_inc(up1_lo, 1)
            pool.wait_ge(bias1_in, 16)
            x1_bias(0)
            with pool.Fori(1, NP) as j:
                for p in range(2):
                    pool.wait_ge(y_done, 2 * j + p - 1)
                    x_lo(2 * j + p, p)
                    x1_bias(2 * j + p - 1)
            x1_bias(NB - 1)

        @block.scalar
        def _(act):
            for p in range(2):
                act.sem_inc(stored[p], 16)
            act.dma_start(consts[:], consts_dram).then_inc(consts_in, 16)
            act.dma_start(bias0[:], bias0_dram).then_inc(bias0_in, 16)
            act.wait_ge(foldT_done, 1)
            nc.scalar.copy(foldT[:], foldT_ps).then_inc(foldT_ready, 1)
            act.wait_ge(fold_done, 1)
            nc.scalar.copy(left0[:, :, :, 0:Q0], fold_ps.rearrange("p (a k) q -> p a k q", a=1)
                           .to_broadcast([P, NP, K, Q0])).then_inc(left0_ready, 1)

            def cond_hi(j, p, half):
                b = 2 * j + p
                if half == 0:
                    act.wait_ge(cond1_in[p], 16 * (j + 1))
                    if not (isinstance(b, int) and b < 2):
                        act.wait_ge(y_done, b - 1)
                ks = slice(half * K // 2, (half + 1) * K // 2)
                nc.scalar.copy(cond1h[p][:, ks], cond1f[p][:, ks]).then_inc(cond1_hi, 1)

            def x_hi(j, p):
                b = 2 * j + p
                if isinstance(b, int) and b < 2:
                    act.wait_ge(x1T_ready, 2)
                else:
                    act.wait_ge(x1T_ready, 2 * NP)
                    act.wait_ge(y_done, b - 1)
                nc.scalar.copy(x1h[p][:], x1T[:, bass.ds(b, 1)].rearrange("p b k t -> p (b k) t")
                               ).then_inc(x1_hi, 1)

            def exp0(h):
                act.wait_ge(low0_ready, h + 1)
                nc.scalar.activation(r0[h]["ex"][:], r0[h]["low"][:], ACT.Exp).then_inc(ex0_ready, 1)

            def q0T_copy(j):
                act.wait_ge(q0T_done, j + 1)
                act.wait_ge(bcol_ready, 1)
                for p in range(2):
                    nc.scalar.activation(q0T[:, j, p], q0T_ps[j][:, p * T:(p + 1) * T], ACT.Identity,
                                         bias=bcol[:], scale=own[:, p:p + 1]).then_inc(q0T_ready, 1)

            def hw0T_copy(h):
                act.wait_ge(hw0T_done, h + 1)
                nc.scalar.copy(hw0T[:, h * HB:(h + 1) * HB],
                               hw0T_ps[h][0:E0 * R, :].rearrange("p (b t) -> p b t", b=HB)).then_inc(hw0T_ready, 1)

            def x1n_copy(b):
                act.wait_ge(x1n_done, b + 1)
                nc.scalar.copy(x1n[:, b], x1n_ps[b % 2][:]).then_inc(x1n_ready, 1)

            act.wait_ge(consts_in, 16)
            exp0(0)
            q0T_copy(2)
            q0T_copy(3)
            hw0T_copy(0)
            cond_hi(0, 0, 0)
            cond_hi(0, 0, 1)
            x_hi(0, 0)
            exp0(1)
            hw0T_copy(1)
            x_hi(0, 1)
            act.wait_ge(mix1_in, 16)
            for h in range(2):
                ks = slice(h * K // 2, (h + 1) * K // 2)
                nc.scalar.copy(mix1h[:, ks], mix1f[:, ks]).then_inc(const1_hi, 1)
            x1n_copy(0)
            x1n_copy(1)
            cond_hi(0, 1, 0)
            cond_hi(0, 1, 1)
            act.wait_ge(up1_in, 16)
            nc.scalar.copy(up1h[:], up1f[:]).then_inc(const1_hi, 1)
            for b in range(2, NB):
                x1n_copy(b)

            def y_copy(b, p):
                act.wait_ge(y_done, b + 1)
                if not (isinstance(b, int) and b < 2):
                    act.wait_ge(yT_done, b - 1)
                nc.scalar.copy(y_sb[p][:], y_ps[:]).then_inc(y_ready, 1)

            def step(j, p, first=False, last=False, split=True):
                b = 2 * j + p
                jn, pn = (j, 1) if p == 0 else (j + 1, 0)
                act.wait_ge(yT_done, b + 1)
                nc.scalar.copy(yTh[p][:], yT_ps[:].rearrange("p (k t) -> p k t", k=K)).then_inc(yT_hi, 1)
                if not first:
                    hwT_hi(b - 1, 1 - p)
                if split:
                    cond_hi(j + 1, p, 0)
                if not last:
                    y_copy(b + 1, pn)
                if split:
                    x_hi(j + 1, p)
                act.wait_ge(low1_ready, b + 1)
                nc.scalar.activation(r1["ex"][:], r1["low"][:], ACT.Exp).then_inc(ex1_ready, 1)
                if not first:
                    store(b - 1, 1 - p)
                if split:
                    cond_hi(j + 1, p, 1)

            def hwT_hi(b, p):
                act.wait_ge(hw1T_done, b + 1)
                nc.scalar.copy(hw1Th[p][:], hw1T_ps[:, 0:T]).then_inc(hw1T_hi, 1)

            def store(b, p):
                act.wait_ge(out_ready, 2 * (b + 1))
                act.dma_start(out_dram[bass.ds(b, 1)].rearrange("b t n -> t (b n)"), out_sb[p][:]
                              ).then_inc(stored[p], 16)

            y_copy(0, 0)
            step(0, 0, first=True)
            step(0, 1)
            with act.Fori(1, NB // 2 - 1) as j:
                step(j, 0)
                step(j, 1)
            step(NB // 2 - 1, 0, split=False)
            step(NB // 2 - 1, 1, split=False, last=True)
            hwT_hi(NB - 1, 1)
            store(NB - 1, 1)
            for p in range(2):
                act.wait_ge(stored[p], 16 * (NB // 2 + 1))

        @block.vector
        def _(dve):
            TT = nc.vector.tensor_tensor
            nc.vector.memset(bcol[:], 0.0).then_inc(bcol_zero, 1)
            dve.wait_ge(lora_in, 16 * NB)
            nc.vector.tensor_copy(loraB[:], lora[:, :, 1].rearrange("p b k r -> p k b r")).then_inc(loraB_ready, 1)
            for p in range(2):
                nc.vector.tensor_copy(left0[:, :, :, LR + p * R:LR + (p + 1) * R], lora[:, p:NB:2, 0]
                                      ).then_inc(left0_ready, 1)
            dve.wait_ge(consts_in, 16)
            nc.vector.tensor_copy(right0[0:LR], eye0[0:LR].rearrange("p (a q) -> p a q", a=1)
                                  .to_broadcast([LR, NP, Q0])).then_inc(right0_ready, 1)
            dve.wait_ge(loraq_done, 1)
            dve.wait_ge(bcol_zero, 1)
            nc.vector.tensor_copy(bcol[0:Q0], bcol_ps).then_inc(bcol_ready, 1)
            for j in range(NP):
                nc.vector.tensor_scalar(right0[LR:P, j], loraq_ps[j * 2 * R:(j + 1) * 2 * R], LORA_SCALE, None,
                                        ALU.mult).then_inc(right0_ready, 1)
            dve.wait_ge(bcol_ready, 1)
            for j in range(2):
                dve.wait_ge(q0T_done, j + 1)
                nc.vector.scalar_tensor_tensor(q0T[:, j], q0T_ps[j].rearrange("p (b t) -> p b t", b=2), bcol[:],
                                               own.rearrange("p (b a) -> p b a", a=1).to_broadcast([P, 2, T]),
                                               ALU.add, ALU.mult).then_inc(q0T_ready, 2)

            def route(r, logits, nb, e, low, chain, at, low_ready, ex_ready, b):
                def after(n):
                    dve.wait_ge(chain, at + n)

                lj = logits.rearrange("p b (a j) -> p b a j", a=1).to_broadcast([T, nb, e, e])
                le = logits.rearrange("p b (e a) -> p b e a", a=1).to_broadcast([T, nb, e, e])
                if nb == 1:
                    pairs = "p b e j -> p (b e) j"
                    lowm = low.rearrange("p (e j) -> p e j", j=e)
                    nar = lambda t: t.rearrange(pairs)
                else:
                    lowm = low.rearrange("p (a m) -> p a m", a=1).to_broadcast([T, nb, e * e])
                    nar = lambda t: t.rearrange("p b e j -> p b (e j)")
                after(0)
                nc.vector.reduce_max(r["top"][:].rearrange("p b a -> p (b a)"), logits, AX.X).then_inc(chain, 1)
                TT(r["gt"][:], lj, le, ALU.is_gt).then_inc(chain, 1)
                TT(r["eq"][:], lj, le, ALU.is_equal).then_inc(chain, 1)
                after(1)
                TT(r["low"][:], logits, r["top"][:].to_broadcast([T, nb, e]), ALU.subtract).then_inc(low_ready, 1)
                after(3)
                TT(nar(r["eqm"][:]), nar(r["eq"][:]), lowm, ALU.mult).then_inc(chain, 1)
                after(4)
                TT(r["ahead"][:], r["gt"][:], r["eqm"][:], ALU.add).then_inc(chain, 1)
                after(5)
                nc.vector.reduce_sum(r["rank"][:].rearrange("p b e -> p (b e)"),
                                     r["ahead"][:].rearrange("p b e j -> p (b e) j"), AX.X).then_inc(chain, 1)
                after(6)
                dve.wait_ge(ex_ready, b + 1)
                nc.vector.scalar_tensor_tensor(r["w"][:], r["rank"][:], 2.0, r["ex"][:], ALU.is_lt, ALU.mult
                                               ).then_inc(chain, 1)
                after(7)
                nc.vector.reduce_sum(r["total"][:].rearrange("p b a -> p (b a)"), r["w"][:], AX.X).then_inc(chain, 1)
                after(8)
                nc.vector.reciprocal(r["inv"][:], r["total"][:]).then_inc(chain, 1)
                after(9)

            def route0(h):
                chain = 11 * h
                dve.wait_ge(q0_done, h + 1)
                nc.vector.tensor_copy(r0[h]["lg"][:], q0_ps[h][:, :, 0:E0]).then_inc(route0_step, 1)
                route(r0[h], r0[h]["lg"][:], HB, E0, low0, route0_step, chain + 1, low0_ready, ex0_ready, h)
                nc.vector.scalar_tensor_tensor(r0[h]["gate"][:], r0[h]["w"][:], FFN0_SCALE,
                                               r0[h]["inv"][:].to_broadcast([T, HB, E0]),
                                               ALU.mult, ALU.mult).then_inc(route0_step, 1)
                dve.wait_ge(route0_step, chain + 11)
                TT(hw0[:, h * HB:(h + 1) * HB].rearrange("p b (e r) -> p b e r", r=R),
                   q0_ps[h][:, :, E0:Q0].rearrange("p b (e r) -> p b e r", r=R),
                   r0[h]["gate"][:].rearrange("p b (e a) -> p b e a", a=1).to_broadcast([T, HB, E0, R]),
                   ALU.mult).then_inc(hw0_ready, 1)

            def cond_lo(b, p, half):
                dve.wait_ge(cond1_hi, 2 * b + half + 1)
                if half == 0 and not (isinstance(b, int) and b < 2):
                    dve.wait_ge(y_done, b - 1)
                ks = slice(half * K // 2, (half + 1) * K // 2)
                TT(cond1l[p][:, ks], cond1f[p][:, ks], cond1h[p][:, ks].bitcast(fp32), ALU.subtract
                   ).then_inc(cond1_lo, 1)

            def x_lo(b, p):
                dve.wait_ge(x1_hi, b + 1)
                TT(x1l[p][:], x1T[:, bass.ds(b, 1)].rearrange("p b k t -> p (b k) t"), x1h[p][:].bitcast(fp32),
                   ALU.subtract).then_inc(x1_lo, 1)

            def x1_pair(j):
                for c in range(2):
                    dve.wait_ge(delta0_done, 2 * j + c + 1)
                    at = lambda t: t[:, 2 * j:2 * j + 2, 2 * c:2 * c + 2].rearrange("p b k t -> p k b t")
                    TT(at(x1T), delta0_ps[c][:].rearrange("p (k b t) -> p k b t", k=2, b=2), at(xT),
                       ALU.add).then_inc(x1T_ready, 1)

            route0(0)
            x1_pair(0)
            cond_lo(0, 0, 0)
            x_lo(0, 0)
            cond_lo(0, 0, 1)
            route0(1)
            x1_pair(1)
            x_lo(1, 1)
            dve.wait_ge(const1_hi, 2)
            TT(mix1l[:, K // 2:K], mix1f[:, K // 2:K], mix1h[:, K // 2:K].bitcast(fp32), ALU.subtract
               ).then_inc(mix1_lo, 1)
            x1_pair(2)
            x1_pair(3)
            cond_lo(1, 1, 0)
            cond_lo(1, 1, 1)

            def hwT_lo(b, p):
                dve.wait_ge(hw1T_hi, b + 1)
                TT(hw1Tl[p][:], hw1T_ps[:, 0:T], hw1Th[p][:].bitcast(fp32), ALU.subtract).then_inc(hw1T_lo, 1)

            def finish(j, p):
                b = 2 * j + p
                dve.wait_ge(out_done, b + 1)
                dve.wait_ge(x1b_ready, b + 1)
                dve.wait_ge(stored[p], 16 * (j + 1))
                res = x1n[:, bass.ds(b, 1)].rearrange("p b n -> p (b n)")
                TT(out_sb[p][:, 0:OA], outA_ps[p][:, Q1:CA], res[:, 0:OA], ALU.add).then_inc(out_ready, 1)
                TT(out_sb[p][:, OA:D], outB_ps[p], res[:, OA:D], ALU.add).then_inc(out_ready, 1)

            ROUTE1 = 10

            def step(j, p, first=False, last=False, split=True):
                b = 2 * j + p
                pn = 1 - p
                dve.wait_ge(yT_hi, b + 1)
                TT(yTl[p][:], yT_ps[:].rearrange("p (k t) -> p k t", k=K), yTh[p][:].bitcast(fp32), ALU.subtract
                   ).then_inc(yT_lo, 1)
                if not first:
                    hwT_lo(b - 1, pn)
                if split:
                    cond_lo(b + 2, p, 0)
                if not first:
                    finish(j if p else j - 1, pn)
                dve.wait_ge(q1_done, b + 1)
                nc.vector.tensor_copy(r1["lg"][:, 0], outA_ps[p][:, 0:E1]).then_inc(route1_step, 1)
                route(r1, r1["lg"][:], 1, E1, low1, route1_step, ROUTE1 * b + 1, low1_ready, ex1_ready, b)
                if not (isinstance(b, int) and b < 2):
                    dve.wait_ge(hw1T_done, b - 1)
                nc.vector.scalar_tensor_tensor(
                    hw1[p][:].rearrange("p (e r) -> p e r", r=R),
                    outA_ps[p][:, E1:Q1].rearrange("p (e r) -> p e r", r=R), r1["inv"][:, 0],
                    r1["w"][:].rearrange("p a e -> p e a").to_broadcast([T, E1, R]), ALU.mult, ALU.mult
                    ).then_inc(hw1_ready, 1)
                if split:
                    cond_lo(b + 2, p, 1)

            step(0, 0, first=True)
            step(0, 1)
            with dve.Fori(1, NB // 2 - 1) as j:
                step(j, 0)
                step(j, 1)
            step(NB // 2 - 1, 0, split=False)
            step(NB // 2 - 1, 1, split=False, last=True)
            hwT_lo(NB - 1, 1)
            finish(NB // 2 - 1, 1)

        @block.tensor
        def _(pe):
            mm = nc.tensor.matmul
            pe.wait_ge(probe0_in, 16)
            for k in range(K):
                pe.wait_ge(base0_in[k], 16)
                last = mm(foldT_ps, probe0[:, k], base0[:, k], start=k == 0, stop=k == K - 1)
            last.then_inc(foldT_done, 1)
            pe.wait_ge(bias0_in, 16)
            for k in range(K):
                mm(bcol_ps, probe0[:, k], bias0[:, k:k + 1], start=k == 0, stop=k == K - 1)
            pe.wait_ge(foldT_ready, 1)
            pe.wait_ge(consts_in, 16)
            for k in range(K):
                last = nc.tensor.transpose(fold_ps[:, k], foldT[:, k * P:(k + 1) * P], ident[0:Q0, 0:Q0])
            last.then_inc(fold_done, 1)
            pe.wait_ge(loraB_ready, 1)
            for k in range(K):
                last = mm(loraq_ps, loraB[:, k].rearrange("p b r -> p (b r)"), probe0[:, k],
                          start=k == 0, stop=k == K - 1)
            last.then_inc(loraq_done, 1)
            pe.wait_ge(pad_zero, 1)
            pe.wait_ge(left0_ready, 3)

            def left_factors(j):
                pe.wait_ge(x_in[j], 16)
                for k in range(K):
                    m = mm(q0T_ps[j], left0[:, j, k], xT[:, 2 * j:2 * j + 2, k], start=k == 0, stop=k == K - 1)
                m.then_inc(q0T_done, 1)

            def right_factors(h):
                pe.wait_ge(right0_ready, 1 + NP)
                for b in range(h * HB, (h + 1) * HB):
                    pe.wait_ge(q0T_ready, b + 1 if h else 2 * (b // 2 + 1))
                    m = mm(q0_ps[h][:, b % HB], q0T[:, b // 2, b % 2], right0[:, b // 2], start=True, stop=True)
                m.then_inc(q0_done, 1)

            def hw0_transpose(h):
                pe.wait_ge(hw0_ready, h + 1)
                for b in range(HB):
                    m = nc.tensor.transpose(hw0T_ps[h][0:E0 * R, b * T:(b + 1) * T], hw0[:, h * HB + b], ident)
                m.then_inc(hw0T_done, 1)

            def x1_transpose(b):
                pe.wait_ge(x1T_ready, 2 * (b // 2 + 1))
                if b >= 2:
                    pe.wait_ge(x1n_ready, b - 1)
                else:
                    pe.wait_ge(q0T_ready, NB)
                for k in range(K):
                    m = nc.tensor.transpose(x1n_ps[b % 2][:, k * P:(k + 1) * P], x1T[:, b, k], ident)
                m.then_inc(x1n_done, 1)

            def delta0(j):
                pe.wait_ge(hw0T_ready, j // 2 + 1)
                for k in range(K):
                    if j > 0 and k % 2 == 0:
                        pe.wait_ge(x1T_ready, 2 * (j - 1) + k // 2 + 1)
                    last = mm(delta0_ps[k // 2][:, k % 2 * 2 * T:(k % 2 + 1) * 2 * T], up0[:, k * P:(k + 1) * P],
                              hw0T[:, 2 * j:2 * j + 2], start=True, stop=True)
                    if k % 2:
                        last.then_inc(delta0_done, 1)

            def y_product(b, p, half):
                if half == 0:
                    pe.wait_ge(x1_lo, b + 1)
                    if not (isinstance(b, int) and b < 1):
                        pe.wait_ge(y_ready, b)
                pe.wait_ge(cond1_lo, 2 * b + half + 1)
                for k in range(half * K // 2, (half + 1) * K // 2):
                    mm(y_ps[:], x1h[p][:, k], cond1h[p][:, k], start=k == 0, stop=False)
                    mm(y_ps[:], x1h[p][:, k], cond1l[p][:, k], start=False, stop=False)
                    last = mm(y_ps[:], x1l[p][:, k], cond1h[p][:, k], start=False, stop=k == K - 1)
                    if k == K - 1:
                        last.then_inc(y_done, 1)

            def hw_transpose(b, p):
                pe.wait_ge(hw1_ready, b + 1)
                if not (isinstance(b, int) and b < 1):
                    pe.wait_ge(hw1T_lo, b)
                nc.tensor.transpose(hw1T_ps[:, 0:T], hw1[p][:], ident).then_inc(hw1T_done, 1)

            def low_rank(b, p):
                pe.wait_ge(hw1T_lo, b + 1)
                for ps, cols in ((outA_ps[p][:, Q1:CA], slice(0, OA)), (outB_ps[p], slice(OA, D))):
                    mm(ps, hw1Th[p][:], up1h[:, cols], start=False, stop=False, skip_group_check=True)
                    mm(ps, hw1Th[p][:], up1l[:, cols], start=False, stop=False, skip_group_check=True)
                    m = mm(ps, hw1Tl[p][:], up1h[:, cols], start=False, stop=True, skip_group_check=True)
                m.then_inc(out_done, 1)

            def step(j, p, first=False, last=False):
                b = 2 * j + p
                pn = 1 - p
                if not last:
                    y_product(b + 1, pn, 0)
                pe.wait_ge(y_ready, b + 1)
                if not first:
                    pe.wait_ge(yT_lo, b)
                for k in range(K):
                    m = nc.tensor.transpose(yT_ps[:, k * T:(k + 1) * T], y_sb[p][:, k * P:(k + 1) * P], ident)
                m.then_inc(yT_done, 1)
                if not first:
                    hw_transpose(b - 1, pn)
                if not last:
                    y_product(b + 1, pn, 1)
                if not first:
                    low_rank(b - 1, pn)
                pe.wait_ge(yT_lo, b + 1)
                if not (isinstance(b, int) and b < 2):
                    pe.wait_ge(out_ready, 2 * (b - 1))
                for ps, cols in ((outA_ps[p], slice(0, CA)), (outB_ps[p], slice(CA, M1))):
                    for k in range(K):
                        mm(ps, yTh[p][:, k], mix1h[:, k, cols], start=k == 0, stop=False, skip_group_check=True)
                        mm(ps, yTh[p][:, k], mix1l[:, k, cols], start=False, stop=False, skip_group_check=True)
                        m = mm(ps, yTl[p][:, k], mix1h[:, k, cols], start=False, stop=k == K - 1,
                               skip_group_check=True)
                    if cols.start == 0:
                        m.then_inc(q1_done, 1)

            left_factors(0)
            left_factors(1)
            right_factors(0)
            left_factors(2)
            left_factors(3)
            hw0_transpose(0)
            pe.wait_ge(up0_in, 16)
            delta0(0)
            right_factors(1)
            x1_transpose(0)
            x1_transpose(1)
            delta0(1)
            hw0_transpose(1)
            pe.wait_ge(hw0T_ready, 2)
            y_product(0, 0, 0)
            y_product(0, 0, 1)
            for j in range(1, NP):
                if j > 1:
                    delta0(j)
                x1_transpose(2 * j)
                x1_transpose(2 * j + 1)
            pe.wait_ge(mix1_lo, 2)
            pe.wait_ge(up1_lo, 1)
            pe.wait_ge(x1n_ready, NB)
            step(0, 0, first=True)
            step(0, 1)
            with pe.Fori(1, NB // 2 - 1) as j:
                step(j, 0)
                step(j, 1)
            step(NB // 2 - 1, 0)
            step(NB // 2 - 1, 1, last=True)
            hw_transpose(NB - 1, 1)
            low_rank(NB - 1, 1)


def kernel(x, itok_B_0_23, itok_B_0_15, L0_cond_W, L0_cond_b, L0_cond_lora_As, L0_cond_lora_Bs, L0_ffn_A, L0_ffn_B,
           L0_ffn_Wr, L1_cond_weight, L1_ffn_W_base, L1_ffn_b_base, L1_ffn_W_gate, L1_ffn_A, L1_ffn_B):
    import numpy as np
    import concourse.bacc as bacc
    from concourse import mybir
    from concourse.bass_utils import run_bass_kernel_spmd

    P = 128

    def rows(a):
        a = np.asarray(a)
        n, d = a.shape
        return np.ascontiguousarray(a.T.reshape(d // P, P, n).transpose(1, 0, 2))

    x = np.asarray(x)
    NB, T, D = x.shape
    K = D // P
    W = np.asarray(L0_cond_W)
    As, Bs = np.asarray(L0_cond_lora_As), np.asarray(L0_cond_lora_Bs)
    S, _, R = As.shape
    A0, B0, Wr = np.asarray(L0_ffn_A), np.asarray(L0_ffn_B), np.asarray(L0_ffn_Wr)
    A1, B1, Wg = np.asarray(L1_ffn_A), np.asarray(L1_ffn_B), np.asarray(L1_ffn_W_gate)
    V = np.asarray(L1_cond_weight)
    E0, E1 = Wr.shape[0], Wg.shape[0]

    def lower(e):
        return np.tile(np.tril(np.ones((e, e), np.float32), -1).reshape(1, e * e), (P, 1))

    own = np.ones((P, 2), np.float32)
    own[P - R:, 0] = 0
    own[P - 2 * R:P - R, 1] = 0

    arrays = {
        "xT": x.reshape(NB, T, K, P).transpose(3, 0, 2, 1),
        "base0": W.reshape(K, P, D).transpose(1, 0, 2),
        "probe0": rows(np.concatenate([Wr, A0.reshape(E0 * R, D)])),
        "bias0": np.asarray(L0_cond_b).reshape(K, P).T,
        "lora": np.stack([As.reshape(S, K, P, R).transpose(0, 2, 1, 3), Bs.reshape(S, R, K, P).transpose(0, 3, 2, 1)], 2),
        "up0": B0.transpose(0, 2, 1).reshape(E0 * R, D),
        "cond1": V.transpose(0, 2, 1).reshape(V.shape[0], K, P, D).transpose(0, 2, 1, 3),
        "mix1": rows(np.concatenate([Wg, A1.reshape(E1 * R, D), np.asarray(L1_ffn_W_base)])),
        "up1": B1.transpose(0, 2, 1).reshape(E1 * R, D),
        "bias1": np.asarray(L1_ffn_b_base).reshape(1, D),
        "slot0": np.asarray(itok_B_0_23).reshape(1, NB),
        "slot1": np.asarray(itok_B_0_15).reshape(1, NB),
        "consts": np.concatenate([np.eye(P, dtype=np.float32),
                                  own, lower(E0), lower(E1), np.eye(P, E0 + E0 * R, dtype=np.float32)], 1),
    }
    nc = bacc.Bacc("TRN2", target_bir_lowering=False, num_devices=1)
    ins, args = {}, []
    for name, a in arrays.items():
        a = np.ascontiguousarray(a)
        ins[f"{name}_dram"] = a
        args.append(nc.dram_tensor(f"{name}_dram", a.shape, mybir.dt.from_np(a.dtype), kind="ExternalInput").ap())
    args.append(nc.dram_tensor("out_dram", (NB, T, D), mybir.dt.float32, kind="ExternalOutput").ap())
    adaln_ffn_kernel(nc, *args)
    r = run_bass_kernel_spmd(nc, [ins], core_ids=[0])
    return r.results[0]["out_dram"]
```

```python
import concourse.bass as bass
from concourse import mybir
from contextlib import ExitStack


def adaln_ffn_kernel(nc, xT_dram, base0_dram, probe0_dram, bias0_dram, lora_dram, up0_dram, cond1_dram,
                     mix1_dram, up1_dram, bias1_dram, slots_dram,
                     consts_dram, out_dram):
    fp32 = mybir.dt.float32
    fp32r = mybir.dt.float32r
    i32 = mybir.dt.int32
    ALU = mybir.AluOpType
    ACT = mybir.ActivationFunctionType
    AX = mybir.AxisListType

    P = 128
    NB, T, D = out_dram.shape
    K = D // P
    E0 = 4
    E1 = 8
    R = 16
    Q0 = E0 + E0 * R
    Q1 = E1 + E1 * R
    M1 = Q1 + D
    CA = M1 // 2
    OA = CA - Q1
    LR = P - 2 * R
    NP = NB // 2
    WARM = 3
    HB = NB // 2
    LORA_SCALE = 2.0
    FFN0_SCALE = 4.0

    ctx = ExitStack()
    with ctx:
        def sb(name, shape, dt=fp32):
            return ctx.enter_context(nc.sbuf_tensor(name, shape, dt))

        def sem(name):
            return ctx.enter_context(nc.semaphore(name))

        xT = sb("xT", [P, NB, K, T])
        x1T = sb("x1T", [P, NB, K, T])
        base0 = sb("base0", [P, K, D])
        probe0 = sb("probe0", [P, K, Q0])
        bias0 = sb("bias0", [P, K])
        lora = sb("lora", [P, NB, 2, K, R])
        loraB = sb("loraB", [P, K, NB, R])
        warm = sb("warm", [P, D])
        up0 = sb("up0", [E0 * R, D])
        slots = sb("slots", [1, 2 * NB], i32)
        C_ID, C_OWN, C_LOW0 = 0, P, P + 2
        C_LOW1 = C_LOW0 + E0 * E0
        C_EYE = C_LOW1 + E1 * E1
        consts = sb("consts", [P, C_EYE + Q0])
        ident = consts[:, C_ID:C_ID + P]
        own = consts[:, C_OWN:C_OWN + 2]
        low0 = consts[:, C_LOW0:C_LOW0 + E0 * E0]
        low1 = consts[:, C_LOW1:C_LOW1 + E1 * E1]
        eye0 = consts[:, C_EYE:C_EYE + Q0]
        foldT = sb("foldT", [Q0, D])
        bcol = sb("bcol", [P, 1])
        left0 = sb("left0", [P, NP, K, P])
        right0 = sb("right0", [P, NP, Q0])
        q0T = sb("q0T", [P, NP, 2, T])
        hw0 = sb("hw0", [T, NB, E0 * R])
        hw0T = sb("hw0T", [E0 * R, NB, T])

        mix1f = sb("mix1f", [P, K, M1])
        mix1h = sb("mix1h", [P, K, M1], fp32r)
        mix1l = sb("mix1l", [P, K, M1], fp32r)
        up1f = sb("up1f", [E1 * R, D])
        up1h = sb("up1h", [E1 * R, D], fp32r)
        up1l = sb("up1l", [E1 * R, D], fp32r)
        bias1 = sb("bias1", [P, D])

        cond1f = [sb(f"cond1f{s}", [P, K, D]) for s in range(2)]
        cond1h = [sb(f"cond1h{s}", [P, K, D], fp32r) for s in range(2)]
        cond1l = [sb(f"cond1l{s}", [P, K, D], fp32r) for s in range(2)]
        x1h = [sb(f"x1h{s}", [P, K, T], fp32r) for s in range(2)]
        x1l = [sb(f"x1l{s}", [P, K, T], fp32r) for s in range(2)]
        y_sb = [sb(f"y_sb{s}", [T, D]) for s in range(2)]
        yTh = [sb(f"yTh{s}", [P, K, T], fp32r) for s in range(2)]
        yTl = [sb(f"yTl{s}", [P, K, T], fp32r) for s in range(2)]
        x1n = sb("x1n", [T, NB, D])
        hw1 = [sb(f"hw1{s}", [T, E1 * R]) for s in range(2)]
        hw1Th = [sb(f"hw1Th{s}", [E1 * R, T], fp32r) for s in range(2)]
        hw1Tl = [sb(f"hw1Tl{s}", [E1 * R, T], fp32r) for s in range(2)]
        out_sb = [sb(f"out_sb{s}", [T, D]) for s in range(2)]

        def route_tiles(tag, nb, e):
            return {n: sb(f"{n}{tag}", [T, nb] + s) for n, s in dict(
                lg=[e], top=[1], low=[e], ex=[e], gt=[e, e], eq=[e, e], eqm=[e, e], ahead=[e, e],
                rank=[e], w=[e], total=[1], inv=[1], gate=[e]).items()}
        r0 = [route_tiles(f"_0{h}", HB, E0) for h in range(2)]
        r1 = route_tiles("_1", 1, E1)

        bank = [ctx.enter_context(nc.psum_tensor(f"bank{i}", [P, 512], fp32)) for i in range(8)]
        foldT_ps = bank[0][0:Q0, :]
        fold_ps = bank[1][:, 0:K * Q0].rearrange("p (k q) -> p k q", k=K)
        loraq_ps = bank[6][:, 0:Q0]
        bcol_ps = bank[6][0:Q0, Q0:Q0 + 1]
        q0T_ps = [bank[i][:, 0:2 * T] for i in (2, 3, 4, 7)]
        q0_ps = [bank[i][:, 0:HB * Q0].rearrange("p (b q) -> p b q", b=HB) for i in (5, 6)]
        hw0T_ps = [bank[1], bank[1]]
        delta0_ps = [[bank[2], bank[3]]] * (NP - 1) + [[bank[5], bank[6]]]
        x1n_ps = [bank[4], bank[7]]
        y_ps = bank[0]
        yT_ps = bank[1]
        hw1T_ps = bank[2]
        outA_ps = [bank[5][:, 0:CA], bank[6][:, 0:CA]]
        outB_ps = [bank[4][:, 0:CA], bank[7][:, 0:CA]]

        slots_in = sem("slots_in")
        probe0_in = sem("probe0_in")
        bias0_in = sem("bias0_in")
        base0_in = [sem(f"base0_in{k}") for k in range(K)]
        x_in = [sem(f"x_in{j}") for j in range(NP)]
        consts_in = sem("consts_in")
        up0_in = sem("up0_in")
        mix1_in = sem("mix1_in")
        up1_in = sem("up1_in")
        bias1_in = sem("bias1_in")
        cond1_in = [sem(f"cond1_in{s}") for s in range(2)]
        pad_zero = sem("pad_zero")
        loraB_ready = sem("loraB_ready")
        foldT_done = sem("foldT_done")
        foldT_ready = sem("foldT_ready")
        fold_done = sem("fold_done")
        left0_ready = sem("left0_ready")
        bcol_zero = sem("bcol_zero")
        warm_zero = sem("warm_zero")
        bcol_ready = sem("bcol_ready")
        loraq_done = sem("loraq_done")
        right0_ready = sem("right0_ready")
        q0T_done = sem("q0T_done")
        q0T_ready = sem("q0T_ready")
        q0_done = sem("q0_done")
        low0_ready = sem("low0_ready")
        ex0_ready = sem("ex0_ready")
        route0_step = sem("route0_step")
        hw0_ready = sem("hw0_ready")
        hw0T_done = sem("hw0T_done")
        hw0T_ready = sem("hw0T_ready")
        delta0_done = sem("delta0_done")
        x1T_ready = sem("x1T_ready")
        x1n_done = sem("x1n_done")
        x1n_ready = sem("x1n_ready")
        x1b_ready = sem("x1b_ready")
        const1_hi = sem("const1_hi")
        mix1_lo = sem("mix1_lo")
        up1_lo = sem("up1_lo")
        cond1_hi = sem("cond1_hi")
        cond1_lo = sem("cond1_lo")
        cond1_last_lo = sem("cond1_last_lo")
        x1_hi = sem("x1_hi")
        x1_lo = sem("x1_lo")
        y_done = sem("y_done")
        y_ready = sem("y_ready")
        yT_done = sem("yT_done")
        yT_hi = sem("yT_hi")
        yT_lo = sem("yT_lo")
        q1_done = sem("q1_done")
        route1_step = sem("route1_step")
        low1_ready = sem("low1_ready")
        ex1_ready = sem("ex1_ready")
        hw1_ready = sem("hw1_ready")
        hw1T_done = sem("hw1T_done")
        hw1T_hi = sem("hw1T_hi")
        hw1T_lo = sem("hw1T_lo")
        out_done = sem("out_done")
        out_ready = sem("out_ready")
        stored = [sem(f"stored{s}") for s in range(2)]

        lora_of = {"sp": range(6, 8), "act": range(0, 3), "pool": range(3, 6)}
        lora_in = {who: sem(f"lora_in_{who}") for who in lora_of}

        def load_lora(eng, who):
            for b in lora_of[who]:
                s = eng.value_load(slots[0:1, b:b + 1], min_val=0, max_val=lora_dram.shape[0] - 1)
                eng.dma_start(lora[:, b], lora_dram[bass.ds(s, 1)].rearrange("s p h k r -> p (s h) k r")
                              ).then_inc(lora_in[who], 16)

        block = ctx.enter_context(nc.Block())

        @block.sync
        def _(sp):
            sp.dma_start(slots[:], slots_dram).then_inc(slots_in, 16)
            sp.dma_start(probe0[:], probe0_dram).then_inc(probe0_in, 16)
            for k in range(K):
                sp.dma_start(base0[:, k], base0_dram[:, k]).then_inc(base0_in[k], 16)
            for j in range(NP):
                if j == 1:
                    sp.wait_ge(slots_in, 16)
                    load_lora(sp, "sp")
                sp.dma_start(xT[:, 2 * j:2 * j + 2], xT_dram[:, 2 * j:2 * j + 2]).then_inc(x_in[j], 16)
            sp.dma_start(up0[:], up0_dram).then_inc(up0_in, 16)

            def load_cond(b, p):
                s = sp.value_load(slots[0:1, bass.ds(NB + b, 1)], min_val=0, max_val=cond1_dram.shape[0] - 1)
                sp.dma_start(cond1f[p][:], cond1_dram[bass.ds(s, 1)].rearrange("s p k n -> p (s k) n")
                             ).then_inc(cond1_in[p], 16)

            load_cond(0, 0)
            sp.dma_start(mix1f[:], mix1_dram).then_inc(mix1_in, 16)
            load_cond(1, 1)
            sp.dma_start(up1f[:], up1_dram).then_inc(up1_in, 16)
            sp.dma_start(bias1[:], bias1_dram.to_broadcast([P, D])).then_inc(bias1_in, 16)
            with sp.Fori(1, NB // 2) as j:
                for p in range(2):
                    sp.wait_ge(cond1_last_lo, 2 * (2 * j + p - 1))
                    sp.wait_ge(cond1_lo, 2 * (2 * j + p - 1))
                    load_cond(2 * j + p, p)

        @block.gpsimd
        def _(pool):
            nc.gpsimd.memset(left0[:, :, :, Q0:LR], 0.0).then_inc(pad_zero, 1)
            pool.wait_ge(slots_in, 16)
            load_lora(pool, "pool")

            def x_lo(b, p):
                pool.wait_ge(x1_hi, b + 1)
                nc.gpsimd.tensor_tensor(x1l[p][:], x1T[:, bass.ds(b, 1)].rearrange("p b k t -> p (b k) t"),
                                        x1h[p][:].bitcast(fp32), ALU.subtract).then_inc(x1_lo, 1)

            def x1_bias(b):
                pool.wait_ge(x1n_ready, b + 1)
                nc.gpsimd.tensor_tensor(x1n[:, bass.ds(b, 1)].rearrange("p b n -> p (b n)"),
                                        x1n[:, bass.ds(b, 1)].rearrange("p b n -> p (b n)"),
                                        bias1[:], ALU.add).then_inc(x1b_ready, 1)

            def cond_lo(b, p):
                pool.wait_ge(cond1_hi, 2 * (b + 1))
                nc.gpsimd.tensor_tensor(cond1l[p][:, K - 1], cond1f[p][:, K - 1], cond1h[p][:, K - 1].bitcast(fp32),
                                        ALU.subtract).then_inc(cond1_last_lo, 2)

            cond_lo(0, 0)
            pool.wait_ge(const1_hi, 1)
            nc.gpsimd.tensor_tensor(mix1l[:, 0:K // 2], mix1f[:, 0:K // 2], mix1h[:, 0:K // 2].bitcast(fp32),
                                    ALU.subtract).then_inc(mix1_lo, 1)
            cond_lo(1, 1)
            pool.wait_ge(const1_hi, 3)
            nc.gpsimd.tensor_tensor(up1l[:], up1f[:], up1h[:].bitcast(fp32), ALU.subtract).then_inc(up1_lo, 1)
            pool.wait_ge(bias1_in, 16)
            x1_bias(0)
            with pool.Fori(1, NP) as j:
                for p in range(2):
                    pool.wait_ge(y_done, 2 * j + p - 1)
                    x_lo(2 * j + p, p)
                    cond_lo(2 * j + p, p)
                    x1_bias(2 * j + p - 1)
            x1_bias(NB - 1)

        @block.scalar
        def _(act):
            for p in range(2):
                act.sem_inc(stored[p], 16)
            act.dma_start(bias0[:], bias0_dram).then_inc(bias0_in, 16)
            act.dma_start(consts[:], consts_dram).then_inc(consts_in, 16)
            act.wait_ge(slots_in, 16)
            load_lora(act, "act")
            act.wait_ge(foldT_done, 1)
            nc.scalar.copy(foldT[:], foldT_ps).then_inc(foldT_ready, 1)
            act.wait_ge(fold_done, 1)
            nc.scalar.copy(left0[:, :, :, 0:Q0], fold_ps.rearrange("p (a k) q -> p a k q", a=1)
                           .to_broadcast([P, NP, K, Q0])).then_inc(left0_ready, 1)

            def cond_hi(j, p, half):
                b = 2 * j + p
                if half == 0:
                    act.wait_ge(cond1_in[p], 16 * (j + 1))
                    if not (isinstance(b, int) and b < 2):
                        act.wait_ge(y_done, b - 1)
                ks = slice(half * K // 2, (half + 1) * K // 2)
                nc.scalar.copy(cond1h[p][:, ks], cond1f[p][:, ks]).then_inc(cond1_hi, 1)

            def x_hi(j, p):
                b = 2 * j + p
                if isinstance(b, int) and b < 2:
                    act.wait_ge(x1T_ready, 2)
                else:
                    act.wait_ge(x1T_ready, 2 * NP)
                    act.wait_ge(y_done, b - 1)
                nc.scalar.copy(x1h[p][:], x1T[:, bass.ds(b, 1)].rearrange("p b k t -> p (b k) t")
                               ).then_inc(x1_hi, 1)

            def exp0(h):
                act.wait_ge(low0_ready, h + 1)
                nc.scalar.activation(r0[h]["ex"][:], r0[h]["low"][:], ACT.Exp).then_inc(ex0_ready, 1)

            def q0T_copy(j):
                act.wait_ge(q0T_done, j + 1)
                act.wait_ge(bcol_ready, 1)
                for p in range(2):
                    nc.scalar.activation(q0T[:, j, p], q0T_ps[j][:, p * T:(p + 1) * T], ACT.Identity,
                                         bias=bcol[:], scale=own[:, p:p + 1]).then_inc(q0T_ready, 1)

            def hw0T_copy(h):
                act.wait_ge(hw0T_done, h + 1)
                nc.scalar.copy(hw0T[:, h * HB:(h + 1) * HB],
                               hw0T_ps[h][0:E0 * R, :].rearrange("p (b t) -> p b t", b=HB)).then_inc(hw0T_ready, 1)

            def x1n_copy(b):
                act.wait_ge(x1n_done, b + 1)
                nc.scalar.copy(x1n[:, b], x1n_ps[b % 2][:]).then_inc(x1n_ready, 1)

            def y_copy(b, p):
                act.wait_ge(y_done, b + 1)
                if not (isinstance(b, int) and b < 2):
                    act.wait_ge(yT_done, b - 1)
                nc.scalar.copy(y_sb[p][:], y_ps[:]).then_inc(y_ready, 1)

            act.wait_ge(consts_in, 16)
            cond_hi(0, 0, 0)
            cond_hi(0, 0, 1)
            exp0(0)
            q0T_copy(2)
            q0T_copy(3)
            hw0T_copy(0)
            act.wait_ge(mix1_in, 16)
            for h in range(2):
                ks = slice(h * K // 2, (h + 1) * K // 2)
                nc.scalar.copy(mix1h[:, ks], mix1f[:, ks]).then_inc(const1_hi, 1)
            x_hi(0, 0)
            x1n_copy(0)
            exp0(1)
            x1n_copy(1)
            y_copy(0, 0)
            hw0T_copy(1)
            x_hi(0, 1)
            cond_hi(0, 1, 0)
            cond_hi(0, 1, 1)
            act.wait_ge(up1_in, 16)
            nc.scalar.copy(up1h[:], up1f[:]).then_inc(const1_hi, 1)
            x1n_copy(2)
            x1n_copy(3)

            def yT_hi_copy(b, p):
                act.wait_ge(yT_done, b + 1)
                nc.scalar.copy(yTh[p][:], yT_ps[:].rearrange("p (k t) -> p k t", k=K)).then_inc(yT_hi, 1)

            def exp1(b):
                act.wait_ge(low1_ready, b + 1)
                nc.scalar.activation(r1["ex"][:], r1["low"][:], ACT.Exp).then_inc(ex1_ready, 1)

            def step(j, p, first=False):
                b = 2 * j + p
                if first:
                    cond_hi(j + 1, p, 0)
                else:
                    hwT_hi(b - 1, 1 - p)
                yT_hi_copy(b, p)
                if first:
                    x_hi(j + 1, p)
                    rest_of_x1n()
                else:
                    cond_hi(j + 1, p, 0)
                y_copy(b + 1, 1 - p)
                if not first:
                    x_hi(j + 1, p)
                exp1(b)
                if not first:
                    store(b - 1, 1 - p)
                cond_hi(j + 1, p, 1)

            def hwT_hi(b, p):
                act.wait_ge(hw1T_done, b + 1)
                nc.scalar.copy(hw1Th[p][:], hw1T_ps[:, 0:T]).then_inc(hw1T_hi, 1)

            def store(b, p):
                act.wait_ge(out_ready, 2 * (b + 1))
                act.dma_start(out_dram[bass.ds(b, 1)].rearrange("b t n -> t (b n)"), out_sb[p][:]
                              ).then_inc(stored[p], 16)

            def rest_of_x1n():
                for b in range(4, NB):
                    x1n_copy(b)

            step(0, 0, first=True)
            step(0, 1)
            with act.Fori(1, NB // 2 - 1) as j:
                step(j, 0)
                step(j, 1)
            hwT_hi(NB - 3, 1)
            yT_hi_copy(NB - 2, 0)
            y_copy(NB - 1, 1)
            store(NB - 3, 1)
            yT_hi_copy(NB - 1, 1)
            exp1(NB - 2)
            hwT_hi(NB - 2, 0)
            exp1(NB - 1)
            hwT_hi(NB - 1, 1)
            store(NB - 2, 0)
            store(NB - 1, 1)
            for p in range(2):
                act.wait_ge(stored[p], 16 * (NB // 2 + 1))

        @block.vector
        def _(dve):
            TT = nc.vector.tensor_tensor
            nc.vector.memset(warm[:], 0.0).then_inc(warm_zero, 1)
            nc.vector.memset(bcol[:], 0.0).then_inc(bcol_zero, 1)
            for who, those in lora_of.items():
                dve.wait_ge(lora_in[who], 16 * len(those))
            nc.vector.tensor_copy(loraB[:], lora[:, :, 1].rearrange("p b k r -> p k b r")).then_inc(loraB_ready, 1)
            for p in range(2):
                nc.vector.tensor_copy(left0[:, :, :, LR + p * R:LR + (p + 1) * R], lora[:, p:NB:2, 0]
                                      ).then_inc(left0_ready, 1)
            dve.wait_ge(consts_in, 16)
            nc.vector.tensor_copy(right0[0:LR], eye0[0:LR].rearrange("p (a q) -> p a q", a=1)
                                  .to_broadcast([LR, NP, Q0])).then_inc(right0_ready, 1)
            dve.wait_ge(loraq_done, 1)
            dve.wait_ge(bcol_zero, 1)
            nc.vector.tensor_copy(bcol[0:Q0], bcol_ps).then_inc(bcol_ready, 1)
            for j in range(NP):
                nc.vector.tensor_scalar(right0[LR:P, j], loraq_ps[j * 2 * R:(j + 1) * 2 * R], LORA_SCALE, None,
                                        ALU.mult).then_inc(right0_ready, 1)
            dve.wait_ge(bcol_ready, 1)
            for j in range(2):
                dve.wait_ge(q0T_done, j + 1)
                nc.vector.scalar_tensor_tensor(q0T[:, j], q0T_ps[j].rearrange("p (b t) -> p b t", b=2), bcol[:],
                                               own.rearrange("p (b a) -> p b a", a=1).to_broadcast([P, 2, T]),
                                               ALU.add, ALU.mult).then_inc(q0T_ready, 2)

            def route(r, logits, nb, e, low, chain, at, low_ready, ex_ready, b):
                def after(n):
                    dve.wait_ge(chain, at + n)

                lj = logits.rearrange("p b (a j) -> p b a j", a=1).to_broadcast([T, nb, e, e])
                le = logits.rearrange("p b (e a) -> p b e a", a=1).to_broadcast([T, nb, e, e])
                if nb == 1:
                    pairs = "p b e j -> p (b e) j"
                    lowm = low.rearrange("p (e j) -> p e j", j=e)
                    nar = lambda t: t.rearrange(pairs)
                else:
                    lowm = low.rearrange("p (a m) -> p a m", a=1).to_broadcast([T, nb, e * e])
                    nar = lambda t: t.rearrange("p b e j -> p b (e j)")
                after(0)
                nc.vector.reduce_max(r["top"][:].rearrange("p b a -> p (b a)"), logits, AX.X).then_inc(chain, 1)
                TT(r["gt"][:], lj, le, ALU.is_gt).then_inc(chain, 1)
                TT(r["eq"][:], lj, le, ALU.is_equal).then_inc(chain, 1)
                after(1)
                TT(r["low"][:], logits, r["top"][:].to_broadcast([T, nb, e]), ALU.subtract).then_inc(low_ready, 1)
                after(3)
                TT(nar(r["eqm"][:]), nar(r["eq"][:]), lowm, ALU.mult).then_inc(chain, 1)
                after(4)
                TT(r["ahead"][:], r["gt"][:], r["eqm"][:], ALU.add).then_inc(chain, 1)
                after(5)
                nc.vector.reduce_sum(r["rank"][:].rearrange("p b e -> p (b e)"),
                                     r["ahead"][:].rearrange("p b e j -> p (b e) j"), AX.X).then_inc(chain, 1)
                after(6)
                dve.wait_ge(ex_ready, b + 1)
                nc.vector.scalar_tensor_tensor(r["w"][:], r["rank"][:], 2.0, r["ex"][:], ALU.is_lt, ALU.mult
                                               ).then_inc(chain, 1)
                after(7)
                nc.vector.reduce_sum(r["total"][:].rearrange("p b a -> p (b a)"), r["w"][:], AX.X).then_inc(chain, 1)
                after(8)
                nc.vector.reciprocal(r["inv"][:], r["total"][:]).then_inc(chain, 1)
                after(9)

            def route0(h):
                chain = 11 * h
                dve.wait_ge(q0_done, 2 * (h + 1))
                nc.vector.tensor_copy(r0[h]["lg"][:], q0_ps[h][:, :, 0:E0]).then_inc(route0_step, 1)
                route(r0[h], r0[h]["lg"][:], HB, E0, low0, route0_step, chain + 1, low0_ready, ex0_ready, h)
                nc.vector.scalar_tensor_tensor(r0[h]["gate"][:], r0[h]["w"][:], FFN0_SCALE,
                                               r0[h]["inv"][:].to_broadcast([T, HB, E0]),
                                               ALU.mult, ALU.mult).then_inc(route0_step, 1)
                dve.wait_ge(route0_step, chain + 11)
                TT(hw0[:, h * HB:(h + 1) * HB].rearrange("p b (e r) -> p b e r", r=R),
                   q0_ps[h][:, :, E0:Q0].rearrange("p b (e r) -> p b e r", r=R),
                   r0[h]["gate"][:].rearrange("p b (e a) -> p b e a", a=1).to_broadcast([T, HB, E0, R]),
                   ALU.mult).then_inc(hw0_ready, 1)

            def cond_lo(b, p, half):
                dve.wait_ge(cond1_hi, 2 * b + half + 1)
                if half == 0 and not (isinstance(b, int) and b < 2):
                    dve.wait_ge(y_done, b - 1)
                ks = slice(half * K // 2, (half + 1) * K // 2 - half)
                TT(cond1l[p][:, ks], cond1f[p][:, ks], cond1h[p][:, ks].bitcast(fp32), ALU.subtract
                   ).then_inc(cond1_lo, 1)

            def x_lo(b, p):
                dve.wait_ge(x1_hi, b + 1)
                TT(x1l[p][:], x1T[:, bass.ds(b, 1)].rearrange("p b k t -> p (b k) t"), x1h[p][:].bitcast(fp32),
                   ALU.subtract).then_inc(x1_lo, 1)

            def x1_pair(j):
                for c in range(2):
                    dve.wait_ge(delta0_done, 2 * j + c + 1)
                    at = lambda t: t[:, 2 * j:2 * j + 2, 2 * c:2 * c + 2].rearrange("p b k t -> p k b t")
                    TT(at(x1T), delta0_ps[j][c][:].rearrange("p (k b t) -> p k b t", k=2, b=2), at(xT),
                       ALU.add).then_inc(x1T_ready, 1)

            route0(0)
            cond_lo(0, 0, 0)
            cond_lo(0, 0, 1)
            x1_pair(0)
            x_lo(0, 0)
            route0(1)
            x1_pair(1)
            x_lo(1, 1)
            cond_lo(1, 1, 0)
            x1_pair(2)
            cond_lo(1, 1, 1)
            dve.wait_ge(const1_hi, 2)
            TT(mix1l[:, K // 2:K], mix1f[:, K // 2:K], mix1h[:, K // 2:K].bitcast(fp32), ALU.subtract
               ).then_inc(mix1_lo, 1)
            x1_pair(3)

            def hwT_lo(b, p):
                dve.wait_ge(hw1T_hi, b + 1)
                TT(hw1Tl[p][:], hw1T_ps[:, 0:T], hw1Th[p][:].bitcast(fp32), ALU.subtract).then_inc(hw1T_lo, 1)

            def finish(j, p):
                b = 2 * j + p
                dve.wait_ge(out_done, b + 1)
                dve.wait_ge(x1b_ready, b + 1)
                dve.wait_ge(stored[p], 16 * (j + 1))
                res = x1n[:, bass.ds(b, 1)].rearrange("p b n -> p (b n)")
                TT(out_sb[p][:, 0:OA], outA_ps[p][:, Q1:CA], res[:, 0:OA], ALU.add).then_inc(out_ready, 1)
                TT(out_sb[p][:, OA:D], outB_ps[p], res[:, OA:D], ALU.add).then_inc(out_ready, 1)

            ROUTE1 = 10

            def yT_low(b, p):
                dve.wait_ge(yT_hi, b + 1)
                TT(yTl[p][:], yT_ps[:].rearrange("p (k t) -> p k t", k=K), yTh[p][:].bitcast(fp32), ALU.subtract
                   ).then_inc(yT_lo, 1)

            def route1(b, p):
                dve.wait_ge(q1_done, b + 1)
                nc.vector.tensor_copy(r1["lg"][:, 0], outA_ps[p][:, 0:E1]).then_inc(route1_step, 1)
                route(r1, r1["lg"][:], 1, E1, low1, route1_step, ROUTE1 * b + 1, low1_ready, ex1_ready, b)
                if not (isinstance(b, int) and b < 2):
                    dve.wait_ge(hw1T_done, b - 1)
                nc.vector.scalar_tensor_tensor(
                    hw1[p][:].rearrange("p (e r) -> p e r", r=R),
                    outA_ps[p][:, E1:Q1].rearrange("p (e r) -> p e r", r=R), r1["inv"][:, 0],
                    r1["w"][:].rearrange("p a e -> p e a").to_broadcast([T, E1, R]), ALU.mult, ALU.mult
                    ).then_inc(hw1_ready, 1)

            def step(j, p, first=False):
                b = 2 * j + p
                if not first:
                    hwT_lo(b - 1, 1 - p)
                yT_low(b, p)
                cond_lo(b + 2, p, 0)
                if not first:
                    finish(j if p else j - 1, 1 - p)
                route1(b, p)
                cond_lo(b + 2, p, 1)

            step(0, 0, first=True)
            step(0, 1)
            with dve.Fori(1, NB // 2 - 1) as j:
                step(j, 0)
                step(j, 1)
            hwT_lo(NB - 3, 1)
            yT_low(NB - 2, 0)
            finish(NB // 2 - 2, 1)
            route1(NB - 2, 0)
            yT_low(NB - 1, 1)
            hwT_lo(NB - 2, 0)
            route1(NB - 1, 1)
            hwT_lo(NB - 1, 1)
            finish(NB // 2 - 1, 0)
            finish(NB // 2 - 1, 1)

        @block.tensor
        def _(pe):
            mm = nc.tensor.matmul
            pe.wait_ge(warm_zero, 1)
            for _ in range(WARM):
                mm(bank[3][:], warm[:, 0:P], warm[:], start=True, stop=True)
            pe.wait_ge(probe0_in, 16)
            for k in range(K):
                pe.wait_ge(base0_in[k], 16)
                last = mm(foldT_ps, probe0[:, k], base0[:, k], start=k == 0, stop=k == K - 1)
            last.then_inc(foldT_done, 1)
            pe.wait_ge(bias0_in, 16)
            for k in range(K):
                mm(bcol_ps, probe0[:, k], bias0[:, k:k + 1], start=k == 0, stop=k == K - 1)
            pe.wait_ge(foldT_ready, 1)
            pe.wait_ge(consts_in, 16)
            for k in range(K):
                last = nc.tensor.transpose(fold_ps[:, k], foldT[:, k * P:(k + 1) * P], ident[0:Q0, 0:Q0])
            last.then_inc(fold_done, 1)
            pe.wait_ge(loraB_ready, 1)
            for k in range(K):
                last = mm(loraq_ps, loraB[:, k].rearrange("p b r -> p (b r)"), probe0[:, k],
                          start=k == 0, stop=k == K - 1)
            last.then_inc(loraq_done, 1)
            pe.wait_ge(pad_zero, 1)
            pe.wait_ge(left0_ready, 3)

            def left_factors(j):
                pe.wait_ge(x_in[j], 16)
                for k in range(K):
                    m = mm(q0T_ps[j], left0[:, j, k], xT[:, 2 * j:2 * j + 2, k], start=k == 0, stop=k == K - 1)
                m.then_inc(q0T_done, 1)

            def right_factors(j):
                pe.wait_ge(right0_ready, 1 + NP)
                for p in range(2):
                    pe.wait_ge(q0T_ready, 2 * (j + 1))
                    m = mm(q0_ps[j // 2][:, (2 * j + p) % HB], q0T[:, j, p], right0[:, j], start=True, stop=True)
                m.then_inc(q0_done, 1)

            def hw0_transpose(h):
                pe.wait_ge(hw0_ready, h + 1)
                if h > 0:
                    pe.wait_ge(hw0T_ready, h)
                for b in range(HB):
                    m = nc.tensor.transpose(hw0T_ps[h][0:E0 * R, b * T:(b + 1) * T], hw0[:, h * HB + b], ident)
                m.then_inc(hw0T_done, 1)

            def x1_transpose(b):
                pe.wait_ge(x1T_ready, 2 * (b // 2 + 1))
                if b >= 2:
                    pe.wait_ge(x1n_ready, b - 1)
                else:
                    pe.wait_ge(q0T_ready, NB)
                for k in range(K):
                    m = nc.tensor.transpose(x1n_ps[b % 2][:, k * P:(k + 1) * P], x1T[:, b, k], ident)
                m.then_inc(x1n_done, 1)

            def delta0(j):
                pe.wait_ge(hw0T_ready, j // 2 + 1)
                for k in range(K):
                    if 0 < j < NP - 1 and k % 2 == 0:
                        pe.wait_ge(x1T_ready, 2 * (j - 1) + k // 2 + 1)
                    last = mm(delta0_ps[j][k // 2][:, k % 2 * 2 * T:(k % 2 + 1) * 2 * T], up0[:, k * P:(k + 1) * P],
                              hw0T[:, 2 * j:2 * j + 2], start=True, stop=True)
                    if k % 2:
                        last.then_inc(delta0_done, 1)

            def y_product(b, p, half):
                if half == 0:
                    pe.wait_ge(x1_lo, b + 1)
                    if not (isinstance(b, int) and b < 1):
                        pe.wait_ge(y_ready, b)
                pe.wait_ge(cond1_lo, 2 * b + half + 1)
                for k in range(half * K // 2, (half + 1) * K // 2):
                    if k == K - 1:
                        pe.wait_ge(cond1_last_lo, 2 * (b + 1))
                    mm(y_ps[:], x1h[p][:, k], cond1h[p][:, k], start=k == 0, stop=False)
                    mm(y_ps[:], x1h[p][:, k], cond1l[p][:, k], start=False, stop=False)
                    last = mm(y_ps[:], x1l[p][:, k], cond1h[p][:, k], start=False, stop=k == K - 1)
                    if k == K - 1:
                        last.then_inc(y_done, 1)

            def hw_transpose(b, p):
                pe.wait_ge(hw1_ready, b + 1)
                if not (isinstance(b, int) and b < 1):
                    pe.wait_ge(hw1T_lo, b)
                nc.tensor.transpose(hw1T_ps[:, 0:T], hw1[p][:], ident).then_inc(hw1T_done, 1)

            def low_rank(b, p):
                pe.wait_ge(hw1T_lo, b + 1)
                for ps, cols in ((outA_ps[p][:, Q1:CA], slice(0, OA)), (outB_ps[p], slice(OA, D))):
                    mm(ps, hw1Th[p][:], up1h[:, cols], start=False, stop=False, skip_group_check=True)
                    mm(ps, hw1Th[p][:], up1l[:, cols], start=False, stop=False, skip_group_check=True)
                    m = mm(ps, hw1Tl[p][:], up1h[:, cols], start=False, stop=True, skip_group_check=True)
                m.then_inc(out_done, 1)

            def y_transpose(b, p, first=False):
                pe.wait_ge(y_ready, b + 1)
                if not first:
                    pe.wait_ge(yT_lo, b)
                for k in range(K):
                    m = nc.tensor.transpose(yT_ps[:, k * T:(k + 1) * T], y_sb[p][:, k * P:(k + 1) * P], ident)
                m.then_inc(yT_done, 1)

            first_cols, second_cols = slice(0, CA), slice(CA, M1)

            def mix_chunk(ps, cols, p, k):
                mm(ps, yTh[p][:, k], mix1h[:, k, cols], start=k == 0, stop=False, skip_group_check=True)
                mm(ps, yTh[p][:, k], mix1l[:, k, cols], start=False, stop=False, skip_group_check=True)
                return mm(ps, yTl[p][:, k], mix1h[:, k, cols], start=False, stop=k == K - 1,
                          skip_group_check=True)

            def banks_free(b):
                if not (isinstance(b, int) and b < 2):
                    pe.wait_ge(out_ready, 2 * (b - 1))

            def mix_first(b, p, between=None):
                pe.wait_ge(yT_lo, b + 1)
                banks_free(b)
                for k in range(K):
                    if between and k == K // 2:
                        between()
                    m = mix_chunk(outA_ps[p], first_cols, p, k)
                m.then_inc(q1_done, 1)

            def mix_second(p):
                for k in range(K):
                    mix_chunk(outB_ps[p], second_cols, p, k)

            def step(j, p, first=False, before=None, between=None, second=True):
                b = 2 * j + p
                pn = 1 - p
                y_product(b + 1, pn, 0)
                if not first:
                    hw_transpose(b - 1, pn)
                y_transpose(b, p, first)
                y_product(b + 1, pn, 1)
                if not first:
                    low_rank(b - 1, pn)
                if before:
                    before()
                mix_first(b, p, between)
                if first:
                    pe.wait_ge(x1n_ready, NB)
                if second:
                    mix_second(p)

            left_factors(0)
            left_factors(1)
            right_factors(0)
            right_factors(1)
            left_factors(2)
            left_factors(3)
            right_factors(2)
            hw0_transpose(0)
            right_factors(3)
            pe.wait_ge(up0_in, 16)
            delta0(0)
            delta0(1)
            x1_transpose(0)
            x1_transpose(1)
            y_product(0, 0, 0)
            y_product(0, 0, 1)
            hw0_transpose(1)
            x1_transpose(2)
            x1_transpose(3)
            delta0(2)
            delta0(3)

            def before_mix():
                for b in range(4, NB - 2):
                    x1_transpose(b)
                pe.wait_ge(mix1_lo, 2)
                pe.wait_ge(up1_lo, 1)
                pe.wait_ge(x1T_ready, 2 * NP)

            def amid_mix():
                for b in range(NB - 2, NB):
                    x1_transpose(b)

            step(0, 0, first=True, before=before_mix, between=amid_mix)
            step(0, 1)
            with pe.Fori(1, NB // 2 - 1) as j:
                step(j, 0)
                step(j, 1)
            step(NB // 2 - 1, 0, second=False)
            y_transpose(NB - 1, 1)
            mix_second(0)
            pe.wait_ge(yT_hi, NB)
            banks_free(NB - 1)
            for k in range(K):
                for part in (mix1h, mix1l):
                    mm(outA_ps[1], yTh[1][:, k], part[:, k, first_cols], start=k == 0 and part is mix1h,
                       stop=False, skip_group_check=True)
            hw_transpose(NB - 2, 0)
            pe.wait_ge(yT_lo, NB)
            for k in range(K):
                m = mm(outA_ps[1], yTl[1][:, k], mix1h[:, k, first_cols], start=False, stop=k == K - 1,
                       skip_group_check=True)
            m.then_inc(q1_done, 1)
            mix_second(1)
            low_rank(NB - 2, 0)
            hw_transpose(NB - 1, 1)
            low_rank(NB - 1, 1)


def kernel(x, itok_B_0_23, itok_B_0_15, L0_cond_W, L0_cond_b, L0_cond_lora_As, L0_cond_lora_Bs, L0_ffn_A, L0_ffn_B,
           L0_ffn_Wr, L1_cond_weight, L1_ffn_W_base, L1_ffn_b_base, L1_ffn_W_gate, L1_ffn_A, L1_ffn_B):
    import numpy as np
    import concourse.bacc as bacc
    from concourse import mybir
    from concourse.bass_utils import run_bass_kernel_spmd

    P = 128

    def rows(a):
        a = np.asarray(a)
        n, d = a.shape
        return np.ascontiguousarray(a.T.reshape(d // P, P, n).transpose(1, 0, 2))

    x = np.asarray(x)
    NB, T, D = x.shape
    K = D // P
    W = np.asarray(L0_cond_W)
    As, Bs = np.asarray(L0_cond_lora_As), np.asarray(L0_cond_lora_Bs)
    S, _, R = As.shape
    A0, B0, Wr = np.asarray(L0_ffn_A), np.asarray(L0_ffn_B), np.asarray(L0_ffn_Wr)
    A1, B1, Wg = np.asarray(L1_ffn_A), np.asarray(L1_ffn_B), np.asarray(L1_ffn_W_gate)
    V = np.asarray(L1_cond_weight)
    E0, E1 = Wr.shape[0], Wg.shape[0]

    def lower(e):
        return np.tile(np.tril(np.ones((e, e), np.float32), -1).reshape(1, e * e), (P, 1))

    own = np.ones((P, 2), np.float32)
    own[P - R:, 0] = 0
    own[P - 2 * R:P - R, 1] = 0

    arrays = {
        "xT": x.reshape(NB, T, K, P).transpose(3, 0, 2, 1),
        "base0": W.reshape(K, P, D).transpose(1, 0, 2),
        "probe0": rows(np.concatenate([Wr, A0.reshape(E0 * R, D)])),
        "bias0": np.asarray(L0_cond_b).reshape(K, P).T,
        "lora": np.stack([As.reshape(S, K, P, R).transpose(0, 2, 1, 3), Bs.reshape(S, R, K, P).transpose(0, 3, 2, 1)], 2),
        "up0": B0.transpose(0, 2, 1).reshape(E0 * R, D),
        "cond1": V.transpose(0, 2, 1).reshape(V.shape[0], K, P, D).transpose(0, 2, 1, 3),
        "mix1": rows(np.concatenate([Wg, A1.reshape(E1 * R, D), np.asarray(L1_ffn_W_base)])),
        "up1": B1.transpose(0, 2, 1).reshape(E1 * R, D),
        "bias1": np.asarray(L1_ffn_b_base).reshape(1, D),
        "slots": np.concatenate([np.asarray(itok_B_0_23), np.asarray(itok_B_0_15)]).reshape(1, 2 * NB),
        "consts": np.concatenate([np.eye(P, dtype=np.float32),
                                  own, lower(E0), lower(E1), np.eye(P, E0 + E0 * R, dtype=np.float32)], 1),
    }
    nc = bacc.Bacc("TRN2", target_bir_lowering=False, num_devices=1)
    ins, args = {}, []
    for name, a in arrays.items():
        a = np.ascontiguousarray(a)
        ins[f"{name}_dram"] = a
        args.append(nc.dram_tensor(f"{name}_dram", a.shape, mybir.dt.from_np(a.dtype), kind="ExternalInput").ap())
    args.append(nc.dram_tensor("out_dram", (NB, T, D), mybir.dt.float32, kind="ExternalOutput").ap())
    adaln_ffn_kernel(nc, *args)
    r = run_bass_kernel_spmd(nc, [ins], core_ids=[0])
    return r.results[0]["out_dram"]
```
